# Optimizing a Trainium2 kernel written in Bass

```python
import numpy as np
import jax
import jax.numpy as jnp

def _softmax(x, axis=-1):
    return jax.nn.softmax(x, axis=axis)

def _gelu(x):
    return jax.nn.gelu(x, approximate=True)

def _silu(x):
    return jax.nn.silu(x)

def _sigmoid(x):
    return jax.nn.sigmoid(x)

def _layernorm(x, axis=-1, eps=1e-05):
    m = jnp.mean(x, axis=axis, keepdims=True)
    v = jnp.var(x, axis=axis, keepdims=True)
    return (x - m) / jnp.sqrt(v + eps)

def _scatter_add(tgt, idx, src, axis=0):
    return tgt.at[idx].add(src)

def _segment_sum(src, seg, n):
    return jax.ops.segment_sum(src, seg, n)
kernel_name = 'mk_gnn_preln_d2_gnn_r32_a035f3'

def setup_inputs(seed: int=0):
    np.random.seed(seed)
    _w = jnp.asarray

    def _rec_inputs():
        import jax
        import jax.numpy as jnp
        _gk = jax.random.key(seed)
        x = -0.000202 + 1 * jax.random.normal(jax.random.fold_in(_gk, 1), (50000, 128), jnp.float32)
        src = jax.random.randint(jax.random.fold_in(_gk, 2), (50000,), 0, 50000, jnp.int32)
        dst = jax.random.randint(jax.random.fold_in(_gk, 3), (50000,), 0, 50000, jnp.int32)
        _o = jnp.argsort(dst, stable=True)
        src = src[_o]
        dst = dst[_o]
        edge_attr_50 = 0.000164634 + 1.0002 * jax.random.normal(jax.random.fold_in(_gk, 11), (50000, 50), jnp.float32)
        edge_weight = jax.random.uniform(jax.random.fold_in(_gk, 13), (50000,), jnp.float32, 0.0, 0.999999)
        return (x, src, dst, edge_attr_50, edge_weight)
    x, src, dst, edge_attr_50, edge_weight = _rec_inputs()

    def _L0_gnn_setup():
        import jax, jax.numpy as jnp
        import numpy as np
        N_NODES = 50000
        N_EDGES = 50000
        D_FEAT = 128
        key = jax.random.key(seed)
        k1, k2, k3 = jax.random.split(key, 3)
        x = jax.random.normal(k1, (N_NODES, D_FEAT), dtype=jnp.float32)
        edge_index = jax.random.randint(k2, (2, N_EDGES), 0, N_NODES, dtype=jnp.int64)
        edge_attr = jax.random.uniform(k3, (N_EDGES,), dtype=jnp.float32)
        return {'x': x, 'edge_index': edge_index, 'edge_attr': edge_attr}
    _L0_gnn_all = _L0_gnn_setup()
    _L0_gnn_in = {k: v for k, v in _L0_gnn_all.items() if k in ()}
    del _L0_gnn_all

    def _L1_gnn_setup():
        import jax, jax.numpy as jnp
        import numpy as np
        N_NODES = 50000
        N_EDGES = 25000
        NODE_DIM = 128
        EDGE_DIM = 50
        HIDDEN_DIM = 128

        def _linear_params(key, fan_in, fan_out):
            kw, kb = jax.random.split(key)
            bound = 1.0 / np.sqrt(fan_in)
            W = jax.random.uniform(kw, (fan_in, fan_out), minval=-bound, maxval=bound, dtype=jnp.float32)
            b = jax.random.uniform(kb, (fan_out,), minval=-bound, maxval=bound, dtype=jnp.float32)
            return (W, b)
        key = jax.random.key(seed)
        ks = jax.random.split(key, 7)
        x = jax.random.normal(ks[0], (N_NODES, NODE_DIM), dtype=jnp.float32)
        edge_index = jax.random.randint(ks[1], (2, N_EDGES), 0, N_NODES, dtype=jnp.int64)
        edge_features = jax.random.normal(ks[2], (N_EDGES, EDGE_DIM), dtype=jnp.float32)
        We1, be1 = _linear_params(ks[3], EDGE_DIM, HIDDEN_DIM)
        We2, be2 = _linear_params(ks[4], HIDDEN_DIM, NODE_DIM)
        Wn1, bn1 = _linear_params(ks[5], NODE_DIM, HIDDEN_DIM)
        Wn2, bn2 = _linear_params(ks[6], HIDDEN_DIM, NODE_DIM)
        return {'x': x, 'edge_index': edge_index, 'edge_features': edge_features, 'We1': We1, 'be1': be1, 'We2': We2, 'be2': be2, 'Wn1': Wn1, 'bn1': bn1, 'Wn2': Wn2, 'bn2': bn2}
    _L1_gnn_all = _L1_gnn_setup()
    _L1_gnn_in = {k: v for k, v in _L1_gnn_all.items() if k in ('We1', 'be1', 'We2', 'be2', 'Wn1', 'bn1', 'Wn2', 'bn2')}
    del _L1_gnn_all
    return {'x': x, 'src': src, 'dst': dst, 'edge_attr_50': edge_attr_50, 'edge_weight': edge_weight, 'L1_gnn_We1': _L1_gnn_in['We1'], 'L1_gnn_be1': _L1_gnn_in['be1'], 'L1_gnn_We2': _L1_gnn_in['We2'], 'L1_gnn_be2': _L1_gnn_in['be2'], 'L1_gnn_Wn1': _L1_gnn_in['Wn1'], 'L1_gnn_bn1': _L1_gnn_in['bn1'], 'L1_gnn_Wn2': _L1_gnn_in['Wn2'], 'L1_gnn_bn2': _L1_gnn_in['bn2']}

def reference(x, src, dst, edge_attr_50, edge_weight, L1_gnn_We1, L1_gnn_be1, L1_gnn_We2, L1_gnn_be2, L1_gnn_Wn1, L1_gnn_bn1, L1_gnn_Wn2, L1_gnn_bn2):
    import jax
    import jax.numpy as jnp

    def _L0_gnn_ref(x, edge_index, edge_attr):
        import jax, jax.numpy as jnp
        import numpy as np
        N_NODES = 50000
        N_EDGES = 50000
        D_FEAT = 128
        row, col = (edge_index[0], edge_index[1])
        num_nodes = x.shape[0]
        deg = jax.ops.segment_sum(jnp.ones_like(edge_attr), row, num_segments=num_nodes)
        deg_inv_sqrt = jnp.where(deg > 0, deg ** (-0.5), 0.0)
        w = deg_inv_sqrt[row] * edge_attr * deg_inv_sqrt[col]
        w = jnp.where(row == col, 0.0, w)
        agg = jax.ops.segment_sum(w[:, None] * x[col], row, num_segments=num_nodes)
        out = agg + (deg_inv_sqrt * deg_inv_sqrt)[:, None] * x
        return out

    def _L1_gnn_ref(x, edge_index, edge_features, We1, be1, We2, be2, Wn1, bn1, Wn2, bn2):
        import jax, jax.numpy as jnp
        import numpy as np
        N_NODES = 50000
        N_EDGES = 25000
        NODE_DIM = 128
        EDGE_DIM = 50
        HIDDEN_DIM = 128

        def _linear_params(key, fan_in, fan_out):
            kw, kb = jax.random.split(key)
            bound = 1.0 / np.sqrt(fan_in)
            W = jax.random.uniform(kw, (fan_in, fan_out), minval=-bound, maxval=bound, dtype=jnp.float32)
            b = jax.random.uniform(kb, (fan_out,), minval=-bound, maxval=bound, dtype=jnp.float32)
            return (W, b)
        src = edge_index[0]
        dst = edge_index[1]
        edge_weights = jax.nn.silu(edge_features @ We1 + be1) @ We2 + be2
        messages = x[src] * edge_weights
        agg = jax.ops.segment_sum(messages, dst, num_segments=x.shape[0])
        out = jax.nn.silu(agg @ Wn1 + bn1) @ Wn2 + bn2
        return x + out
    edge_index = jnp.stack([src, dst])
    h = jnp.maximum(_layernorm(x, axis=-1), 0.0)
    x = x + _L0_gnn_ref(h, edge_index, edge_weight)
    h = jnp.maximum(_layernorm(x, axis=-1), 0.0)
    x = x + _L1_gnn_ref(h, edge_index, edge_attr_50, L1_gnn_We1, L1_gnn_be1, L1_gnn_We2, L1_gnn_be2, L1_gnn_Wn1, L1_gnn_bn1, L1_gnn_Wn2, L1_gnn_bn2)
    return x

_drawn_inputs = setup_inputs


def setup_inputs(seed=0):
    import zlib

    import numpy as np

    out = dict(_drawn_inputs(seed))
    spreads = {}
    factors = {'edge_attr_50': 5.057,
     'L1_gnn_We1': 5.007,
     'L1_gnn_be1': 8.0,
     'L1_gnn_We2': 4.81,
     'L1_gnn_be2': 28.136,
     'L1_gnn_Wn1': 4.574,
     'L1_gnn_bn1': 59.328,
     'L1_gnn_Wn2': 3.973,
     'L1_gnn_bn2': 64.0}
    for name, (base, spread) in spreads.items():
        noise = np.random.default_rng([zlib.crc32(name.encode()), seed]).standard_normal(out[name].shape)
        drawn = base * np.exp(spread * noise) if base else spread * noise
        out[name] = jnp.asarray(drawn.astype(out[name].dtype))
    for name, factor in factors.items():
        out[name] = (out[name] * factor).astype(out[name].dtype)
    return out
```

```python
import concourse.bass as bass
from concourse import mybir
from contextlib import ExitStack

ALU = mybir.AluOpType
ACT = mybir.ActivationFunctionType
F32 = mybir.dt.float32
F16 = mybir.dt.float16
BF16 = mybir.dt.bfloat16
I32 = mybir.dt.int32

N = 50000
D = 128
DE = 50
P = 128
T = N // P
TAIL = N - P * T
K = 10
NG = T // K
PAIRS = K // 2
ZW = 132
EPS = 1e-5
MAGIC = float(0x5F3759DF)
NEWTON = 3
LN_STEPS = 20
assert NG * K == T and NG % 2 == 1 and K % 2 == 0


class Steps:

    def __init__(self, sem):
        self.eng, self.sem, self.start, self.n = None, sem, 0, 0

    def link(self, instruction):
        instruction.then_inc(self.sem, 1)
        self.n += 1
        self.eng.wait_ge(self.sem, self.start + self.n)

    def enter(self, i, per_turn):
        self.before = self.start + self.n
        self.start, self.n, self.per_turn = i * per_turn + self.before, 0, per_turn

    def leave(self, turns):
        assert self.n == self.per_turn, (self.n, self.per_turn)
        self.start, self.n = self.before + turns * self.per_turn, 0


def build(nc, x, src, dst, edge_attr, edge_weight, we1, be1, we2, be2, wn1, bn1, wn2, bn2, out):
    main = P * T
    with ExitStack() as ctx:
        def sb(name, shape, dt=F32):
            return ctx.enter_context(nc.sbuf_tensor(name, shape, dt))

        def sem(name):
            return ctx.enter_context(nc.semaphore(name))

        g_table = nc.dram_tensor("g_table", (N, D), F32).ap()
        z_table = nc.dram_tensor("z_table", (N + P, ZW), F32).ap()
        m_table = nc.dram_tensor("m_table", (N + P, D), F32).ap()

        def rows(table, width):
            return table[0:main, :].rearrange("(p t) d -> p t d", t=T)[:, :, 0:width]

        src_i, dst_i = sb("src_i", [P, T + 1], I32), sb("dst_i", [P, T + 1], I32)
        src_f, dst_f = sb("src_f", [P, T + 1]), sb("dst_f", [P, T + 1])
        src_hi, src_lo = sb("src_hi", [P, T + 1], BF16), sb("src_lo", [P, T + 1], BF16)
        dst_hi, dst_lo = sb("dst_hi", [P, T + 1], BF16), sb("dst_lo", [P, T + 1], BF16)
        ew = sb("ew", [P, T + 1])
        d_all, r_all, s_all, dis_all = (sb(n, [P, T + 1]) for n in ("d_all", "r_all", "s_all", "dis_all"))
        ident, ident16, ident256 = sb("ident", [P, P]), sb("ident16", [P, P], BF16), sb("ident256", [P, P], BF16)
        before = sb("before", [P, 3 * P])
        spare_row = sb("spare_row", [P, 1])
        zeros = sb("zeros", [P, K * D])
        ones_row = sb("ones_row", [1, P])
        w1e, w2e, w1n, w2n = sb("w1e", [DE, D]), sb("w2e", [D, D]), sb("w1n", [D, D]), sb("w2n", [D, D])
        b1e, b1n = sb("b1e", [D, 1]), sb("b1n", [D, 1])
        b2e, b2n = sb("b2e", [1, 2 * D]), sb("b2n", [1, 2 * D])
        steps = Steps(sem("dve_steps"))

        def rsqrt(y, v, t):
            v_, y_, t_ = v.bitcast(I32), y.bitcast(I32), t.bitcast(I32)
            steps.link(nc.vector.tensor_scalar(t_, v_, 1, None, ALU.logical_shift_right))
            steps.link(nc.vector.tensor_scalar(y_, t_, -1.0, MAGIC, ALU.mult, ALU.add))
            for _ in range(NEWTON):
                steps.link(nc.vector.tensor_tensor(t, y, y, ALU.mult))
                steps.link(nc.vector.tensor_tensor(t, t, v, ALU.mult))
                steps.link(nc.vector.tensor_scalar(t, t, -0.5, 1.5, ALU.mult, ALU.add))
                steps.link(nc.vector.tensor_tensor(y, y, t, ALU.mult))

        def layernorm_coefficients(tiles, d, dis, st, small, scale, shift):
            k = len(tiles)
            n = tiles[0].shape[0]
            for j, tile in enumerate(tiles):
                last = nc.vector.bn_stats(st[0:n, j, :], tile)
            steps.link(last)
            total, diff, var, room = (small[0:n, m, 0:k] for m in range(4))
            even, odd = st[0:n, 0:k, 0:3], st[0:n, 0:k, 3:6]
            nc.vector.tensor_tensor(total, even[:, :, 1], odd[:, :, 1], ALU.add)
            nc.vector.tensor_tensor(var, even[:, :, 2], odd[:, :, 2], ALU.add)
            steps.link(nc.vector.tensor_tensor(diff, even[:, :, 1], odd[:, :, 1], ALU.subtract))
            if d is None:
                steps.link(nc.vector.tensor_scalar(var, var, 1.0 / D, EPS, ALU.mult, ALU.add))
            else:
                nc.vector.tensor_scalar(room, d, EPS, None, ALU.mult)
                steps.link(nc.vector.tensor_scalar(var, var, 1.0 / D, None, ALU.mult))
                steps.link(nc.vector.tensor_tensor(var, var, room, ALU.add))
            steps.link(nc.vector.tensor_tensor(diff, diff, diff, ALU.mult))
            steps.link(nc.vector.scalar_tensor_tensor(out=var, in0=diff, scalar=0.25, in1=var, op0=ALU.mult, op1=ALU.add))
            rsqrt(scale, var, room)
            if dis is not None:
                steps.link(nc.vector.tensor_tensor(scale, scale, dis, ALU.mult))
            return nc.vector.scalar_tensor_tensor(out=shift, in0=total, scalar=-0.5, in1=scale,
                                                  op0=ALU.mult, op1=ALU.mult)

        with ExitStack() as ph:
            hot_q = ph.enter_context(nc.sbuf_tensor("hot_q", [P, K, P], BF16))
            hot_r = ph.enter_context(nc.sbuf_tensor("hot_r", [P, K, T + 1], BF16))
            iota_q = ph.enter_context(nc.sbuf_tensor("iota_q", [P, P], F16))
            iota_r = ph.enter_context(nc.sbuf_tensor("iota_r", [P, T + 1], F16))
            q = ph.enter_context(nc.sbuf_tensor("q", [P, T + 1], F32))
            r = ph.enter_context(nc.sbuf_tensor("r", [P, T + 1], F32))
            t1 = ph.enter_context(nc.sbuf_tensor("t1", [P, T + 1], F32))
            i1 = ph.enter_context(nc.sbuf_tensor("i1", [P, T + 1], I32))
            i2 = ph.enter_context(nc.sbuf_tensor("i2", [P, T + 1], I32))
            qr = ph.enter_context(nc.sbuf_tensor("qr", [P, 2, K], F32))
            deg = ph.enter_context(nc.psum_tensor("deg", [P, 512], F32))
            edges_in, weights_in = ph.enter_context(nc.semaphore("edges_in")), sem("weights_in")
            pads_set, consts_set = ph.enter_context(nc.semaphore("pads_set")), sem("consts_set")
            hots_ready = ph.enter_context(nc.semaphore("hots_ready"))
            hots_used = ph.enter_context(nc.semaphore("hots_used"))
            block = ph.enter_context(nc.Block())
            PADS = 3

            @block.sync
            def _(sp):
                sp.wait_ge(pads_set, PADS)
                for held, edges in ((src_i, src), (dst_i, dst), (ew, edge_weight)):
                    sp.dma_start(held[:, 0:T], edges[0:main].rearrange("(p t) -> p t", t=T)).then_inc(edges_in, 16)
                    sp.dma_start(held[0:TAIL, T:T + 1], edges[main:N].rearrange("(p t) -> p t", t=1)).then_inc(edges_in, 16)
                for held, w in ((w1e, we1), (w2e, we2), (w1n, wn1), (w2n, wn2)):
                    sp.dma_start(held[:, :], w[:, :]).then_inc(weights_in, 16)
                for held, b in ((b1e, be1), (b1n, bn1)):
                    sp.dma_start(held[:, :], b.rearrange("(p t) -> p t", t=1)).then_inc(weights_in, 16)
                for held, b in ((b2e, be2), (b2n, bn2)):
                    for half in range(2):
                        sp.dma_start(held[:, half * D:(half + 1) * D],
                                     b.rearrange("(p t) -> p t", p=1)).then_inc(weights_in, 16)
                sp.wait_ge(weights_in, 16 * 10)

            @block.gpsimd
            def _(pool):
                for held in (src_i, dst_i, ew):
                    nc.gpsimd.memset(held[:, T:T + 1], 0).then_inc(pads_set, 1)
                nc.gpsimd.iota(iota_q[:, :], [[1, P]], base=0, channel_multiplier=0,
                               allow_small_or_imprecise_dtypes=True).then_inc(consts_set, 1)
                nc.gpsimd.iota(iota_r[:, :], [[1, T + 1]], base=0, channel_multiplier=0,
                               allow_small_or_imprecise_dtypes=True).then_inc(consts_set, 1)
                nc.gpsimd.iota(spare_row[:, :], [[0, 1]], base=N, channel_multiplier=1,
                               allow_small_or_imprecise_dtypes=True).then_inc(consts_set, 1)
                nc.gpsimd.memset(zeros[:, :], 0.0).then_inc(consts_set, 1)
                nc.gpsimd.memset(ones_row[:, :], 1.0).then_inc(consts_set, 1)
                nc.gpsimd.memset(before[:, :], 1.0).then_inc(consts_set, 1)
                for m in (ident, ident16, ident256):
                    nc.gpsimd.memset(m[:, :], 0.0).then_inc(consts_set, 1)
                pool.wait_ge(consts_set, 9)
                for m, one in ((ident, 1.0), (ident16, 1.0), (ident256, 256.0)):
                    nc.gpsimd.affine_select(out=m[:, :], in_=m[:, :], compare_op=ALU.not_equal, fill=one, base=0,
                                            pattern=[[-1, P]], channel_multiplier=1).then_inc(consts_set, 1)
                for at in (0, 2 * P):
                    nc.gpsimd.affine_select(out=before[:, at:at + P], in_=before[:, at:at + P], compare_op=ALU.is_gt,
                                            fill=0.0, base=0, pattern=[[-1, P]],
                                            channel_multiplier=1).then_inc(consts_set, 1)

            @block.vector
            def _(dve):
                steps.eng = dve
                dve.wait_ge(edges_in, 16 * 6)
                nc.vector.tensor_copy(src_f[:, :], src_i[:, :])
                steps.link(nc.vector.tensor_copy(dst_f[:, :], dst_i[:, :]))
                steps.link(nc.vector.tensor_scalar(i1[:, :], src_f[:, :], 1.0 / T, None, ALU.mult))
                steps.link(nc.vector.tensor_copy(q[:, :], i1[:, :]))
                steps.link(nc.vector.scalar_tensor_tensor(out=r[:, :], in0=q[:, :], scalar=-float(T), in1=src_f[:, :],
                                                          op0=ALU.mult, op1=ALU.add))
                for op, bound, sign in ((ALU.is_lt, 0.0, -1.0), (ALU.is_ge, float(T), 1.0)):
                    steps.link(nc.vector.tensor_scalar(t1[:, :], r[:, :], bound, sign, op, ALU.mult))
                    nc.vector.tensor_tensor(q[:, :], q[:, :], t1[:, :], ALU.add)
                    steps.link(nc.vector.scalar_tensor_tensor(out=r[:, :], in0=t1[:, :], scalar=-float(T),
                                                              in1=r[:, :], op0=ALU.mult, op1=ALU.add))
                steps.link(nc.vector.tensor_scalar(t1[:, :], src_f[:, :], float(main), None, ALU.is_ge))
                steps.link(nc.vector.scalar_tensor_tensor(out=d_all[:, :], in0=r[:, :], scalar=-float(P), in1=t1[:, :],
                                                          op0=ALU.add, op1=ALU.mult))
                steps.link(nc.vector.tensor_tensor(q[:, :], q[:, :], d_all[:, :], ALU.add))
                steps.link(nc.vector.scalar_tensor_tensor(out=d_all[:, :], in0=r[:, :], scalar=-float(T), in1=t1[:, :],
                                                          op0=ALU.add, op1=ALU.mult))
                steps.link(nc.vector.tensor_tensor(r[:, :], r[:, :], d_all[:, :], ALU.subtract))
                dve.wait_ge(consts_set, 14)

                def hots(tiles, n, at_q, at_r):
                    for j in tiles:
                        nc.vector.tensor_scalar(hot_q[0:n, j, :], iota_q[0:n, :], at_q[0:n, j:j + 1], None,
                                                ALU.is_equal)
                        last = nc.vector.tensor_scalar(hot_r[0:n, j, :], iota_r[0:n, :], at_r[0:n, j:j + 1],
                                                       None, ALU.is_equal)
                    last.then_inc(hots_ready, 1)

                with dve.Fori(0, NG) as g:
                    steps.enter(g, 2)
                    for half in range(2):
                        dve.wait_ge(hots_used, g * 2 + (half + 1))
                        at, now = slice(half * K // 2, (half + 1) * K // 2), bass.ds(g * K + half * K // 2, K // 2)
                        nc.vector.tensor_copy(qr[:, 0, at], q[:, now])
                        steps.link(nc.vector.tensor_copy(qr[:, 1, at], r[:, now]))
                        hots(range(half * K // 2, (half + 1) * K // 2), P, qr[:, 0, :], qr[:, 1, :])
                steps.leave(NG)
                dve.wait_ge(hots_used, NG * 2 + 1)
                hots([0], TAIL, q[:, T:T + 1], r[:, T:T + 1])

                for whole, high, low in ((src_i, src_hi, src_lo), (dst_i, dst_hi, dst_lo)):
                    nc.vector.tensor_scalar(i1[:, :], whole[:, :], 8, None, ALU.logical_shift_right)
                    steps.link(nc.vector.tensor_scalar(i2[:, :], whole[:, :], 255, None, ALU.bitwise_and))
                    nc.vector.tensor_copy(high[:, :], i1[:, :])
                    steps.link(nc.vector.tensor_copy(low[:, :], i2[:, :]))
                steps.link(nc.vector.tensor_tensor(t1[:, :], src_f[:, :], dst_f[:, :], ALU.not_equal))
                steps.link(nc.vector.tensor_tensor(ew[:, :], ew[:, :], t1[:, :], ALU.mult))
                dve.wait_ge(hots_used, NG * 2 + 3)
                nc.vector.tensor_scalar(t1[:, :], deg[:, 0:T + 1], 1.0, None, ALU.min)
                steps.link(nc.vector.tensor_scalar(d_all[:, :], deg[:, 0:T + 1], 1.0, None, ALU.max))
                rsqrt(r_all[:, :], d_all[:, :], q[:, :])
                nc.vector.tensor_tensor(s_all[:, :], d_all[:, :], r_all[:, :], ALU.mult)
                steps.link(nc.vector.tensor_tensor(dis_all[:, :], t1[:, :], r_all[:, :], ALU.mult))

            @block.tensor
            def _(pe):
                pe.wait_ge(consts_set, 14)
                nc.tensor.matmul(deg[:, 0:T + 1], ident16[:, :], zeros[:, 0:T + 1].bitcast(BF16)[:, 0:T + 1],
                                 start=True, stop=False, skip_group_check=True)

                pe.sem_inc(hots_used, 2)

                def count(tiles, n, last_of_all=False):
                    for j in tiles:
                        last = nc.tensor.matmul(deg[:, 0:T + 1], hot_q[0:n, j, :], hot_r[0:n, j, :],
                                                start=False, stop=last_of_all, skip_group_check=True)
                    last.then_inc(hots_used, 1)

                with pe.Fori(0, NG) as g:
                    for half in range(2):
                        pe.wait_ge(hots_ready, g * 2 + (half + 1))
                        count(range(half * K // 2, (half + 1) * K // 2), P)
                pe.wait_ge(hots_ready, NG * 2 + 1)
                count([0], TAIL, last_of_all=True)

        with ExitStack() as ph:
            def buf(name, shape, dt=F32):
                return ph.enter_context(nc.sbuf_tensor(name, shape, dt))

            def flag(name):
                return ph.enter_context(nc.semaphore(name))

            xt = buf("xt", [P, 2, K, D])
            gt = buf("gt", [P, 2, K, D])
            zt = buf("zt", [P, 2, K, ZW])
            st = buf("st2", [P, K, 6])
            small = buf("small2", [P, 4, K])
            coef = buf("coef2", [P, 2, 2, K])
            s_now = buf("s_now", [P, K])
            x_in = [flag(f"x_in{b}") for b in range(2)]
            coef_ready, g_ready, z_ready = flag("coef_ready2"), flag("g_ready"), flag("z_ready")
            stored = [flag(f"stored{b}") for b in range(2)]
            block = ph.enter_context(nc.Block())

            @block.sync
            def _(sp):
                def load(g, b):
                    sp.wait_ge(z_ready, g + 1)
                    sp.dma_start(xt[:, b, :, :], rows(x, D)[:, bass.ds(g * K, K), :]).then_inc(x_in[b], 16)

                with sp.Fori(0, NG // 2) as i:
                    for b in range(2):
                        load(i * 2 + b, b)
                load(NG - 1, 0)
                sp.wait_ge(z_ready, NG + 1)
                sp.dma_start(xt[0:TAIL, 1, 0, :], x[main:N, :]).then_inc(x_in[1], 16)

            @block.vector
            def _(dve):
                steps.eng = dve
                dve.sem_inc(z_ready, 2)
                nc.vector.memset(zt[:, 0, :, D + 1:ZW], 0.0)
                steps.link(nc.vector.memset(zt[:, 1, :, D + 1:ZW], 0.0))

                def group(g, i, b, k, n):
                    cols = bass.ds(g * K, k)
                    dve.wait_ge(x_in[b], i * 16 + 16)
                    last = layernorm_coefficients([xt[0:n, b, j, :] for j in range(k)], None, dis_all[0:n, cols], st,
                                                  small, coef[0:n, b, 0, 0:k], coef[0:n, b, 1, 0:k])
                    last.then_inc(coef_ready, 1)
                    dve.wait_ge(stored[b], i * 32 + 16)
                    nc.vector.tensor_copy(zt[0:n, b, 0:k, D], d_all[0:n, cols])
                    steps.link(nc.vector.tensor_copy(s_now[0:n, 0:k], s_all[0:n, cols]))
                    dve.wait_ge(g_ready, g + 1)
                    for j in range(k):
                        last = nc.vector.scalar_tensor_tensor(
                            out=zt[0:n, b, j, 0:D], in0=xt[0:n, b, j, :], scalar=s_now[0:n, j:j + 1],
                            in1=gt[0:n, b, j, :], op0=ALU.mult, op1=ALU.add)
                    last.then_inc(z_ready, 1)

                with dve.Fori(0, NG // 2) as i:
                    steps.enter(i, 2 * (LN_STEPS + 1))
                    for b in range(2):
                        group(i * 2 + b, i, b, K, P)
                steps.leave(NG // 2)
                group(NG - 1, NG // 2, 0, K, P)
                group(NG, NG // 2, 1, 1, TAIL)

            @block.scalar
            def _(act):
                def group(g, i, b, k, n):
                    act.wait_ge(coef_ready, g + 1)
                    act.wait_ge(stored[b], i * 32 + 16)
                    for j in range(k):
                        last = nc.scalar.activation(gt[0:n, b, j, :], xt[0:n, b, j, :], ACT.Relu,
                                                    scale=coef[0:n, b, 0, j:j + 1], bias=coef[0:n, b, 1, j:j + 1])
                    last.then_inc(g_ready, 1)

                with act.Fori(0, NG // 2) as i:
                    for b in range(2):
                        group(i * 2 + b, i, b, K, P)
                group(NG - 1, NG // 2, 0, K, P)
                group(NG, NG // 2, 1, 1, TAIL)

            @block.gpsimd
            def _(pool):
                pool.dma_start(z_table[N:N + P, :], zeros[:, 0:ZW]).then_inc(stored[0], 16)
                pool.dma_start(m_table[main:N, :], zeros[0:TAIL, 0:D]).then_inc(stored[1], 16)

                def store(g, b):
                    pool.wait_ge(z_ready, g + 3)
                    pool.dma_start(rows(g_table, D)[:, bass.ds(g * K, K), :], gt[:, b, :, :]).then_inc(stored[b], 16)
                    pool.dma_start(rows(z_table, ZW)[:, bass.ds(g * K, K), :], zt[:, b, :, :]).then_inc(stored[b], 16)

                with pool.Fori(0, NG // 2) as i:
                    for b in range(2):
                        store(i * 2 + b, b)
                store(NG - 1, 0)
                pool.wait_ge(z_ready, NG + 3)
                pool.dma_start(g_table[main:N, :], gt[0:TAIL, 1, 0, :]).then_inc(stored[1], 16)
                pool.dma_start(z_table[main:N, :], zt[0:TAIL, 1, 0, :]).then_inc(stored[1], 16)
                for b in range(2):
                    pool.wait_ge(stored[b], 32 * (NG + 1) // 2 + 16)

        def edge_layer(layer):
            mlp = layer == 2
            table, width, gather_i = (z_table, ZW, src_i) if mlp else (g_table, D, dst_i)
            key_f, key_hi, key_lo = (dst_f, dst_hi, dst_lo) if mlp else (src_f, src_hi, src_lo)
            sums_table, sum_width = (m_table, D) if mlp else (z_table, ZW)
            with ExitStack() as ph:
                def buf(name, shape, dt=F32):
                    return ph.enter_context(nc.sbuf_tensor(f"{name}_{layer}", shape, dt))

                def bank(name, shape):
                    return ph.enter_context(nc.psum_tensor(f"{name}_{layer}", shape, F32))

                def flag(name):
                    return ph.enter_context(nc.semaphore(f"{name}_{layer}"))

                got = buf("got", [P, 2, K, width])
                sums = buf("sums", [P, 2, K, sum_width])
                same = buf("same", [P, 2, PAIRS, 3 * P])
                dup = buf("dup", [P, K])
                junk = buf("junk", [P, 2, 3 * P], BF16)
                gather_at, sums_at = buf("gather_at", [P, 2, K], I32), buf("sums_at", [P, 2, K], I32)
                key, weight = buf("key", [P, 2, K]), buf("weight", [P, 2, K])
                hi, lo = buf("hi", [P, 2, K], BF16), buf("lo", [P, 2, K], BF16)
                detour = buf("detour", [P, K])
                key_row = [bank(f"key_row{b}", [P, 2 * P]) for b in range(2)]
                pair_sums = [bank(f"pair_sums{b}", [P, 2 * P]) for b in range(2)]
                staged = flag("staged")
                gathered = [flag(f"gathered{b}") for b in range(2)]
                keys_spread = flag("keys_spread")
                compared = flag("compared")
                rows_picked = flag("rows_picked")
                summed = flag("summed")
                sums_ready = flag("sums_ready")
                sums_added = flag("sums_added")
                waited = flag("waited")
                added = flag("added")
                if mlp:
                    ea = buf("ea", [P, 2, K, DE])
                    eat = buf("eat", [DE, 2, 2 * P])
                    hidden = buf("hidden", [P, 2 * P])
                    normed = buf("normed", [P, 2, K, D])
                    message = buf("message", [P, 2, 2, D])
                    st, small, coef = buf("st", [P, K, 6]), buf("small", [P, 4, K]), buf("coef", [P, 2, 2, K])
                    d_now = buf("d_now", [P, K])
                    eat_p = [bank(f"eat_p{b}", [DE, 2 * P]) for b in range(2)]
                    hidden_p, filter_p = bank("hidden_p", [P, 2 * P]), bank("filter_p", [P, 2 * P])
                    ea_in = [flag(f"ea_in{b}") for b in range(2)]
                    turned, eat_ready = flag("turned"), flag("eat_ready")
                    hid_summed, hid_ready = flag("hid_summed"), flag("hid_ready")
                    filter_ready, message_ready = flag("filter_ready"), flag("message_ready")
                    coef_ready, normed_ready = flag("coef_ready"), flag("normed_ready")
                else:
                    cleared, fill_set = flag("cleared"), flag("fill_set")
                block = ph.enter_context(nc.Block())

                def halves(tiles):
                    return [range(j, min(j + 2, tiles)) for j in range(0, tiles, 2)]

                def groups(eng, group):
                    with eng.Fori(0, NG // 2) as i:
                        for b in range(2):
                            group(i * 2 + b, i, b, K, P)
                    group(NG - 1, NG // 2, 0, K, P)
                    group(NG, NG // 2, 1, 1, TAIL)

                def size(g, n):
                    return (1, TAIL) if isinstance(g, int) and g == NG - 1 else (K, P)

                @block.sync
                def _(sp):
                    if mlp:
                        attr = edge_attr[0:main, :].rearrange("(p t) d -> p t d", t=T)

                        def load(g, b):
                            sp.wait_ge(turned, g * PAIRS + 1)
                            sp.dma_start(ea[:, b, :, :], attr[:, bass.ds(g * K, K), :]).then_inc(ea_in[b], 16)

                        with sp.Fori(0, NG // 2) as i:
                            for b in range(2):
                                load(i * 2 + b, b)
                        load(NG - 1, 0)
                        sp.wait_ge(turned, NG * PAIRS + 1)
                        sp.dma_start(ea[0:TAIL, 1, 0, :], edge_attr[main:N, :]).then_inc(ea_in[1], 16)
                    else:
                        sp.dma_start(rows(m_table, D)[:, 0:K, :],
                                     zeros[:, :].rearrange("p (k d) -> p k d", d=D)).then_inc(cleared, 16)
                        with sp.Fori(1, NG) as g:
                            sp.wait_ge(cleared, g * 16)
                            sp.dma_start(rows(m_table, D)[:, bass.ds(g * K, K), :],
                                         zeros[:, :].rearrange("p (k d) -> p k d", d=D)).then_inc(cleared, 16)
                        sp.wait_ge(cleared, 16 * NG)

                @block.gpsimd
                def _(pool):
                    pool.sem_inc(added, K - 1)
                    at = N + (P // 2 if mlp else 0)
                    pool.dma_start(m_table[at:at + P // 2, :], zeros[0:P // 2, 0:D]).then_inc(sums_added, 16)

                    def gather(b, j, n):
                        pool.indirect_dma_start(got[0:n, b, j, :], None, table[:, :],
                                                bass.IndirectOffsetOnAxis(gather_at[0:n, b, j:j + 1], axis=0)
                                                ).then_inc(gathered[b], 16)

                    def group(g, i, b, tiles, n):
                        ahead, ahead_n = (0, 0) if tiles == 1 else size(g, n)
                        for k, pair in enumerate(halves(tiles)):
                            if k == 0 and ahead:
                                pool.wait_ge(staged, g + 2)
                                if mlp:
                                    pool.wait_ge(normed_ready, g + 1)
                                else:
                                    pool.wait_ge(summed, g * PAIRS + (PAIRS + 1))
                                pool.sem_inc(waited, 1)
                            for j in pair:
                                if j < ahead:
                                    gather(1 - b, j, ahead_n)
                            pool.wait_ge(sums_added, (g * PAIRS + k) * 32 + 16)
                            pool.sem_inc(added, 1)
                            if k == 0:
                                pool.wait_ge(rows_picked, g + 2)
                            pool.wait_ge(sums_ready, g * PAIRS + (k + 3))
                            pool.sem_inc(waited, 1)
                            for j in pair:
                                pool.indirect_dma_start(
                                    sums_table[:, :], bass.IndirectOffsetOnAxis(sums_at[0:n, b, j:j + 1], axis=0),
                                    sums[0:n, b, j, :], None, compute_op=ALU.add).then_inc(sums_added, 16)

                    pool.wait_ge(staged, 1)
                    for j in range(K):
                        gather(0, j, P)
                    groups(pool, group)
                    pool.wait_ge(sums_added, 16 * (T + 2))

                @block.vector
                def _(dve):
                    steps.eng = dve
                    dve.sem_inc(compared, 2)
                    dve.sem_inc(rows_picked, 1)
                    if mlp:
                        dve.sem_inc(message_ready, 1)

                    def stage(g, b, tiles, n):
                        cols = bass.ds(g * K, tiles)
                        for held, whole in ((key, key_f), (hi, key_hi), (lo, key_lo)) + (() if mlp else ((weight, ew),)):
                            nc.vector.tensor_copy(held[0:n, b, 0:tiles], whole[0:n, cols])
                        nc.vector.tensor_copy(gather_at[0:n, b, 0:tiles], gather_i[0:n, cols]).then_inc(staged, 1)

                    def group(g, i, b, tiles, n):
                        if tiles == K:
                            dve.wait_ge(rows_picked, g + 1)
                            if not mlp:
                                dve.wait_ge(summed, g * PAIRS + (PAIRS + 1))
                            stage(g + 1, 1 - b, *size(g, n))
                        dve.wait_ge(staged, g + 1)
                        if mlp:
                            dve.wait_ge(gathered[b], i * 16 * K + 16 * tiles)
                            steps.link(nc.vector.tensor_copy(d_now[0:n, 0:tiles], got[0:n, b, 0:tiles, D]))
                            last = layernorm_coefficients([got[0:n, b, j, 0:D] for j in range(tiles)],
                                                          d_now[0:n, 0:tiles], None, st, small,
                                                          coef[0:n, b, 0, 0:tiles], coef[0:n, b, 1, 0:tiles])
                            last.then_inc(coef_ready, 1)
                        dve.wait_ge(summed, g * PAIRS + 1)
                        for k, pair in enumerate(halves(tiles)):
                            dve.wait_ge(keys_spread, g * PAIRS + (k + 1))
                            dve.wait_ge(compared, g * PAIRS + (k + 1))
                            spread = key_row[(b + k) % 2]
                            for m, j in enumerate(pair):
                                others = n if tiles == 1 else (m + 1) * P
                                at = m * P
                                mine = key[0:n, b, j:j + 1]
                                w = (None, None) if mlp else (weight[0:n, b, j:j + 1], ALU.mult)
                                nc.vector.tensor_scalar(same[0:n, b, k, at:at + others], spread[0:n, 0:others], mine,
                                                        w[0], ALU.is_equal, *([w[1]] if w[1] else []))
                                last = nc.vector.scalar_tensor_tensor(
                                    out=junk[0:n, (b + k) % 2, at:at + others], in0=spread[0:n, 0:others], scalar=mine,
                                    in1=before[0:n, at:at + others], op0=ALU.is_equal, op1=ALU.mult,
                                    accum_out=dup[0:n, j:j + 1])
                            last.then_inc(compared, 1)
                            if mlp:
                                dve.wait_ge(filter_ready, g * PAIRS + (k + 2))
                                dve.wait_ge(normed_ready, g + 2)
                                dve.wait_ge(summed, g * PAIRS + (k + PAIRS))
                                nc.vector.tensor_tensor(
                                    message[0:n, (b + k) % 2, 0:len(pair), :], normed[0:n, b, pair[0]:pair[-1] + 1, :],
                                    filter_p[0:n, 0:len(pair) * D].rearrange("p (j d) -> p j d", d=D),
                                    ALU.mult).then_inc(message_ready, 1)
                        dve.wait_ge(compared, g * PAIRS + (len(halves(tiles)) + 2))
                        mine, many = key[0:n, b, 0:tiles], dup[0:n, 0:tiles]
                        steps.link(nc.vector.tensor_scalar(detour[0:n, 0:tiles], mine, -1.0, spare_row[0:n, :],
                                                           ALU.mult, ALU.add))
                        steps.link(nc.vector.scalar_tensor_tensor(out=detour[0:n, 0:tiles], in0=many, scalar=1.0,
                                                                  in1=detour[0:n, 0:tiles], op0=ALU.min, op1=ALU.mult))
                        dve.wait_ge(added, g * PAIRS + PAIRS)
                        nc.vector.tensor_tensor(sums_at[0:n, b, 0:tiles], mine, detour[0:n, 0:tiles],
                                                ALU.add).then_inc(rows_picked, 1)

                    stage(0, 0, K, P)
                    with dve.Fori(0, NG // 2) as i:
                        steps.enter(i, 2 * (2 + (LN_STEPS + 1 if mlp else 0)))
                        for b in range(2):
                            group(i * 2 + b, i, b, K, P)
                    steps.leave(NG // 2)
                    group(NG - 1, NG // 2, 0, K, P)
                    group(NG, NG // 2, 1, 1, TAIL)

                @block.scalar
                def _(act):
                    act.sem_inc(sums_ready, 2)
                    if mlp:
                        act.sem_inc(eat_ready, 2)
                        act.sem_inc(hid_ready, 1)
                        act.sem_inc(normed_ready, 1)
                    else:
                        for b in range(2):
                            nc.scalar.activation(sums[:, b, :, D:ZW], zeros[:, 0:K * (ZW - D)].rearrange(
                                "p (k d) -> p k d", k=K), ACT.Copy).then_inc(fill_set, 1)
                        act.wait_ge(fill_set, 2)

                    def turn(p, b, n, count):
                        act.wait_ge(turned, p + (PAIRS + 2))
                        act.wait_ge(hid_summed, p + 1)
                        nc.scalar.activation(eat[:, b, 0:count * n], eat_p[b][:, 0:count * n],
                                             ACT.Copy).then_inc(eat_ready, 1)

                    def group(g, i, b, tiles, n):
                        if mlp:
                            act.wait_ge(coef_ready, g + 1)
                            for j in range(tiles):
                                last = nc.scalar.activation(
                                    normed[0:n, b, j, :], got[0:n, b, j, 0:D], ACT.Relu,
                                    scale=coef[0:n, b, 0, j:j + 1], bias=coef[0:n, b, 1, j:j + 1])
                            last.then_inc(normed_ready, 1)
                        for k, pair in enumerate(halves(tiles)):
                            p = g * PAIRS + k
                            count = len(pair)
                            if mlp:
                                last_pair = tiles == 1
                                if not last_pair:
                                    one = tiles == K and k == PAIRS - 1 and size(g, n)[0] == 1
                                    turn(p + 1, (b + k + 1) % 2, TAIL if one else P, 1 if one else 2)
                                act.wait_ge(hid_summed, p + 3)
                                act.wait_ge(filter_ready, p + 1)
                                nc.scalar.activation(hidden[:, 0:count * n], hidden_p[:, 0:count * n], ACT.Silu,
                                                     bias=b1e[:, 0:1]).then_inc(hid_ready, 1)
                            act.wait_ge(summed, p + (PAIRS + 2))
                            act.wait_ge(added, p + 1)
                            nc.scalar.activation(
                                sums[0:n, b, pair[0]:pair[-1] + 1, 0:D],
                                pair_sums[(b + k) % 2][0:n, 0:count * D].rearrange("p (j d) -> p j d", d=D),
                                ACT.Copy).then_inc(sums_ready, 1)

                    if mlp:
                        turn(0, 0, P, 2)
                    groups(act, group)

                @block.tensor
                def _(pe):
                    pe.sem_inc(summed, PAIRS + 1)
                    if mlp:
                        pe.sem_inc(turned, PAIRS + 1)
                        pe.sem_inc(hid_summed, 2)
                        pe.sem_inc(filter_ready, 1)

                    def spread(g, p, i, b, k, tiles, n):
                        if k == 0:
                            pe.wait_ge(staged, g + 1)
                        pe.wait_ge(compared, p + 1)
                        if mlp:
                            if k == 0:
                                pe.wait_ge(ea_in[b], i * 16 + 16)
                            pe.wait_ge(eat_ready, p + 1)
                        pair = halves(tiles)[k]
                        for m, j in enumerate(pair):
                            cols = slice(m * P, m * P + n)
                            nc.tensor.matmul(key_row[(b + k) % 2][0:n, cols], hi[0:n, b, j:j + 1].to_broadcast([n, n]),
                                             ident256[0:n, 0:n], start=True, stop=False)
                            last = nc.tensor.matmul(key_row[(b + k) % 2][0:n, cols],
                                                    lo[0:n, b, j:j + 1].to_broadcast([n, n]),
                                                    ident16[0:n, 0:n], start=False, stop=True)
                        last.then_inc(keys_spread, 1)
                        if mlp:
                            for m, j in enumerate(pair):
                                last = nc.tensor.transpose(eat_p[(b + k) % 2][:, m * P:m * P + n], ea[0:n, b, j, :],
                                                           ident[0:n, 0:n])
                            last.then_inc(turned, 1)

                    def group(g, i, b, tiles, n):
                        for k, pair in enumerate(halves(tiles)):
                            p = g * PAIRS + k
                            count = len(pair)
                            if k < PAIRS - 1 and tiles == K:
                                spread(g, p + 1, i, b, k + 1, K, P)
                            elif tiles == K:
                                spread(g + 1, p + 1, i + b, 1 - b, 0, *size(g, n))
                            if mlp:
                                pe.wait_ge(eat_ready, p + 3)
                                pe.wait_ge(hid_ready, p + 1)
                                nc.tensor.matmul(hidden_p[:, 0:count * n], w1e[:, :], eat[:, (b + k) % 2, 0:count * n],
                                                 start=True, stop=True).then_inc(hid_summed, 1)
                                pe.wait_ge(message_ready, p + 1)
                                nc.tensor.matmul(filter_p[0:n, 0:count * D], ones_row[:, 0:n], b2e[:, 0:count * D],
                                                 start=True, stop=False, skip_group_check=True)
                                pe.wait_ge(hid_ready, p + 2)
                                for m in range(count):
                                    last = nc.tensor.matmul(filter_p[0:n, m * D:(m + 1) * D], hidden[:, m * n:(m + 1) * n],
                                                            w2e[:, :], start=False, stop=(m == count - 1),
                                                            skip_group_check=True)
                                last.then_inc(filter_ready, 1)
                                pe.wait_ge(message_ready, p + 2)
                                data = [message[0:n, (b + k) % 2, m, :] for m in range(count)]
                            else:
                                if k == 0:
                                    pe.wait_ge(gathered[b], i * 16 * K + 16 * tiles)
                                data = [got[0:n, b, j, :] for j in pair]
                            pe.wait_ge(compared, p + 3)
                            pe.wait_ge(sums_ready, p + 1)
                            bank_ = pair_sums[(b + k) % 2]
                            same_ = same[0:n, b, k, :]
                            last = nc.tensor.matmul(bank_[0:n, 0:D], same_[:, 0:n], data[0], start=True, stop=(count == 1))
                            if count == 2:
                                nc.tensor.matmul(bank_[:, 0:D], same_[:, P:2 * P], data[1], start=False, stop=True)
                                last = nc.tensor.matmul(bank_[:, D:2 * D], same_[:, 2 * P:3 * P], data[1],
                                                        start=True, stop=True)
                            last.then_inc(summed, 1)

                    spread(0, 0, 0, 0, 0, K, P)
                    groups(pe, group)

        edge_layer(1)
        edge_layer(2)

        with ExitStack() as ph:
            def buf(name, shape, dt=F32):
                return ph.enter_context(nc.sbuf_tensor(name, shape, dt))

            def flag(name):
                return ph.enter_context(nc.semaphore(name))

            def bank(name):
                return ph.enter_context(nc.psum_tensor(name, [P, 2 * P], F32))

            zn, mn, on = buf("zn", [P, 2, K, ZW]), buf("mn", [P, 2, K, D]), buf("on", [P, 2, K, D])
            h2 = buf("h2", [P, 2, K, D])
            st, small, coef = buf("st5", [P, K, 6]), buf("small5", [P, 4, K]), buf("coef5", [P, 2, 2, K])
            r_now = buf("r_now", [P, 2, K])
            mt, hidden, branch = buf("mt", [P, 2, 2 * P]), buf("hidden5", [P, 2, 2 * P]), buf("branch", [P, 2, 2 * P])
            mt_p, hidden_p, out_p = ([bank(f"{name}{b}") for b in range(2)] for name in ("mt_p", "hid_p", "out_p"))
            rows_in, rows_out = [flag(f"rows_in{b}") for b in range(2)], [flag(f"rows_out{b}") for b in range(2)]
            coef_ready, h_ready = flag("coef5_ready"), flag("h_ready")
            turned, mt_ready, hid_summed, hid_ready = flag("turned5"), flag("mt_ready"), flag("hid5_summed"), flag("hid5_ready")
            branch_summed, branch_added, out_ready = flag("branch_summed"), flag("branch_added"), flag("out_ready")
            block = ph.enter_context(nc.Block())

            def halves(tiles):
                return [range(j, min(j + 2, tiles)) for j in range(0, tiles, 2)]

            def groups(eng, group):
                with eng.Fori(0, NG // 2) as i:
                    for b in range(2):
                        group(i * 2 + b, i, b, K, P)
                group(NG - 1, NG // 2, 0, K, P)
                group(NG, NG // 2, 1, 1, TAIL)

            @block.sync
            def _(sp):
                def group(g, i, b, tiles, n):
                    sp.wait_ge(out_ready, g + 1)
                    if tiles == 1:
                        z, m = z_table[main:N, :], m_table[main:N, :]
                        sp.dma_start(zn[0:n, b, 0, :], z).then_inc(rows_in[b], 16)
                        sp.dma_start(mn[0:n, b, 0, :], m).then_inc(rows_in[b], 16)
                    else:
                        sp.dma_start(zn[:, b, :, :], rows(z_table, ZW)[:, bass.ds(g * K, K), :]).then_inc(rows_in[b], 16)
                        sp.dma_start(mn[:, b, :, :], rows(m_table, D)[:, bass.ds(g * K, K), :]).then_inc(rows_in[b], 16)

                groups(sp, group)

            @block.gpsimd
            def _(pool):
                def group(g, i, b, tiles, n):
                    pool.wait_ge(out_ready, g + 3)
                    if tiles == 1:
                        pool.dma_start(out[main:N, :], on[0:n, b, 0, :]).then_inc(rows_out[b], 16)
                    else:
                        pool.dma_start(rows(out, D)[:, bass.ds(g * K, K), :], on[:, b, :, :]).then_inc(rows_out[b], 16)

                for b in range(2):
                    pool.dma_start(z_table[N + b:N + b + 1, :], zeros[0:1, 0:ZW]).then_inc(rows_out[b], 16)
                groups(pool, group)
                for b in range(2):
                    pool.wait_ge(rows_out[b], 16 * (NG + 1) // 2 + 16)

            @block.vector
            def _(dve):
                steps.eng = dve
                dve.sem_inc(out_ready, 2)
                dve.sem_inc(branch_added, 2)

                def group(g, i, b, tiles, n):
                    cols = bass.ds(g * K, tiles)
                    dve.wait_ge(rows_in[b], i * 32 + 32)
                    nc.vector.tensor_copy(r_now[0:n, b, 0:tiles], r_all[0:n, cols])
                    last = layernorm_coefficients([zn[0:n, b, j, 0:D] for j in range(tiles)], d_all[0:n, cols], None,
                                                  st, small, coef[0:n, b, 0, 0:tiles], coef[0:n, b, 1, 0:tiles])
                    last.then_inc(coef_ready, 1)
                    dve.wait_ge(h_ready, g + 1)
                    dve.wait_ge(rows_out[b], i * 16 + 16)
                    for k, pair in enumerate(halves(tiles)):
                        dve.wait_ge(branch_summed, g * PAIRS + (k + 2))
                        nc.vector.tensor_tensor(
                            branch[0:n, k % 2, 0:len(pair) * D].rearrange("p (j d) -> p j d", d=D),
                            out_p[(b + k) % 2][0:n, 0:len(pair) * D].rearrange("p (j d) -> p j d", d=D),
                            h2[0:n, b, pair[0]:pair[-1] + 1, :], ALU.add).then_inc(branch_added, 1)
                        dve.wait_ge(branch_added, g * PAIRS + (k + 3))
                        for m, j in enumerate(pair):
                            last = nc.vector.scalar_tensor_tensor(
                                out=on[0:n, b, j, :], in0=zn[0:n, b, j, 0:D], scalar=r_now[0:n, b, j:j + 1],
                                in1=branch[0:n, k % 2, m * D:(m + 1) * D], op0=ALU.mult, op1=ALU.add)
                    last.then_inc(out_ready, 1)

                with dve.Fori(0, NG // 2) as i:
                    steps.enter(i, 2 * LN_STEPS)
                    for b in range(2):
                        group(i * 2 + b, i, b, K, P)
                steps.leave(NG // 2)
                group(NG - 1, NG // 2, 0, K, P)
                group(NG, NG // 2, 1, 1, TAIL)

            @block.scalar
            def _(act):
                def group(g, i, b, tiles, n):
                    act.wait_ge(coef_ready, g + 1)
                    for j in range(tiles):
                        last = nc.scalar.activation(h2[0:n, b, j, :], zn[0:n, b, j, 0:D], ACT.Relu,
                                                    scale=coef[0:n, b, 0, j:j + 1], bias=coef[0:n, b, 1, j:j + 1])
                    last.then_inc(h_ready, 1)
                    for k, pair in enumerate(halves(tiles)):
                        p, c = g * PAIRS + k, len(pair) * n
                        s = (b + k) % 2
                        act.wait_ge(turned, p + 1)
                        act.wait_ge(hid_summed, p + 1)
                        nc.scalar.activation(mt[:, s, 0:c], mt_p[s][:, 0:c], ACT.Copy).then_inc(mt_ready, 1)
                        act.wait_ge(hid_summed, p + 3)
                        act.wait_ge(branch_summed, p + 1)
                        nc.scalar.activation(hidden[:, s, 0:c], hidden_p[s][:, 0:c], ACT.Silu,
                                             bias=b1n[:, 0:1]).then_inc(hid_ready, 1)

                groups(act, group)

            @block.tensor
            def _(pe):
                pe.sem_inc(hid_summed, 2)
                pe.sem_inc(branch_summed, 1)

                def turn(p, i, b, k, tiles, n):
                    if k == 0:
                        pe.wait_ge(rows_in[b], i * 32 + 32)
                    for m, j in enumerate(halves(tiles)[k]):
                        last = nc.tensor.transpose(mt_p[(b + k) % 2][:, m * P:m * P + n], mn[0:n, b, j, :],
                                                   ident[0:n, 0:n])
                    last.then_inc(turned, 1)

                def group(g, i, b, tiles, n):
                    for k, pair in enumerate(halves(tiles)):
                        p, c = g * PAIRS + k, len(pair) * n
                        s = (b + k) % 2
                        turn(p, i, b, k, tiles, n)
                        pe.wait_ge(mt_ready, p + 1)
                        nc.tensor.matmul(hidden_p[s][:, 0:c], w1n[:, :], mt[:, s, 0:c],
                                         start=True, stop=True).then_inc(hid_summed, 1)
                        pe.wait_ge(branch_added, p + 1)
                        nc.tensor.matmul(out_p[s][0:n, 0:len(pair) * D], ones_row[:, 0:n], b2n[:, 0:len(pair) * D],
                                         start=True, stop=False, skip_group_check=True)
                        pe.wait_ge(hid_ready, p + 1)
                        for m in range(len(pair)):
                            last = nc.tensor.matmul(out_p[s][0:n, m * D:(m + 1) * D], hidden[:, s, m * n:(m + 1) * n],
                                                    w2n[:, :], start=False, stop=(m == len(pair) - 1),
                                                    skip_group_check=True)
                        last.then_inc(branch_summed, 1)

                groups(pe, group)


INPUTS = ["x", "src", "dst", "edge_attr_50", "edge_weight", "L1_gnn_We1", "L1_gnn_be1", "L1_gnn_We2", "L1_gnn_be2",
          "L1_gnn_Wn1", "L1_gnn_bn1", "L1_gnn_Wn2", "L1_gnn_bn2"]


def kernel(**inputs):
    import numpy as np
    import concourse.bacc as bacc
    from concourse.bass_utils import run_bass_kernel_spmd

    nc = bacc.Bacc("TRN2", target_bir_lowering=False, num_devices=1)
    arrays, args = {}, []
    for name in INPUTS:
        a = np.ascontiguousarray(inputs[name])
        arrays[f"in_{name}"] = a
        args.append(nc.dram_tensor(f"in_{name}", a.shape, mybir.dt.from_np(a.dtype), kind="ExternalInput").ap())
    args.append(nc.dram_tensor("out", (N, D), F32, kind="ExternalOutput").ap())
    build(nc, *args)
    return run_bass_kernel_spmd(nc, [arrays], core_ids=[0]).results[0]["out"]
```

```python
import concourse.bass as bass
from concourse import mybir
from contextlib import ExitStack

ALU = mybir.AluOpType
ACT = mybir.ActivationFunctionType
F32 = mybir.dt.float32
F16 = mybir.dt.float16
BF16 = mybir.dt.bfloat16
I32 = mybir.dt.int32

N = 50000
D = 128
DE = 50
P = 128
Q = 32
T = N // P
TAIL = N - P * T
K = 10
NG = T // K
PAIRS = K // 2
KN, NGN = 30, T // 30
C = 3
ZW = 132
EPS = 1e-5
MAGIC = float(0x5F3759DF)
NEWTON = 3
LN_STEPS = 18
assert NG * K == T and NG % 2 == 1 and PAIRS > 2
assert NGN * KN == T and NGN % 3 == 1 and KN % (2 * C) == 0


class Steps:

    def __init__(self, sem):
        self.eng, self.sem, self.start, self.n = None, sem, 0, 0

    def link(self, instruction):
        instruction.then_inc(self.sem, 1)
        self.n += 1
        self.eng.wait_ge(self.sem, self.start + self.n)

    def enter(self, i, per_turn):
        self.before = self.start + self.n
        self.start, self.n, self.per_turn = i * per_turn + self.before, 0, per_turn

    def leave(self, turns):
        assert self.n == self.per_turn, (self.n, self.per_turn)
        self.start, self.n = self.before + turns * self.per_turn, 0


def build(nc, x, src, dst, src_by_tile, dst_by_tile, attr_t, edge_weight, we1, be1, we2, be2, wn1, bn1, wn2, bn2, out):
    main = P * T
    with ExitStack() as ctx:
        def sb(name, shape, dt=F32):
            return ctx.enter_context(nc.sbuf_tensor(name, shape, dt))

        def sem(name):
            return ctx.enter_context(nc.semaphore(name))

        g_table = nc.dram_tensor("g_table", (N, D), F32).ap()
        z_table = nc.dram_tensor("z_table", (N + P, ZW), F32).ap()
        m_table = nc.dram_tensor("m_table", (N + P, D), F32).ap()

        def rows(table):
            return table[0:main, :].rearrange("(p t) d -> p t d", t=T)

        src_i, dst_i = sb("src_i", [P, T + 1], I32), sb("dst_i", [P, T + 1], I32)
        src_f, dst_f = sb("src_f", [P, T + 1]), sb("dst_f", [P, T + 1])
        ew = sb("ew", [P, T + 1])
        d_all, r_all, s_all, dis_all = (sb(n, [P, T + 1]) for n in ("d_all", "r_all", "s_all", "dis_all"))
        ident = sb("ident", [P, P])
        before = sb("before", [P, 3 * P])
        spare_row = sb("spare_row", [P, 1])
        zeros = sb("zeros", [P, K * D])
        w1e, w2e, w1n, w2n = sb("w1e", [DE, D]), sb("w2e", [D, D]), sb("w1n", [D, D]), sb("w2n", [D, D])
        b1e, b1n = sb("b1e", [D, 1]), sb("b1n", [D, 1])
        b2e, b2n = sb("b2e", [3 * Q, D]), sb("b2n", [3 * Q, D])
        b2e_terms, b2n_terms = sb("b2e_terms", [3 * Q, C * D], BF16), sb("b2n_terms", [3 * Q, C * D], BF16)
        first_rows = sb("first_rows", [3 * Q, P], BF16)
        steps = Steps(sem("dve_steps"))

        def rsqrt(y, v, t):
            v_, y_, t_ = v.bitcast(I32), y.bitcast(I32), t.bitcast(I32)
            steps.link(nc.vector.tensor_scalar(t_, v_, 1, None, ALU.logical_shift_right))
            steps.link(nc.vector.tensor_scalar(y_, t_, -1.0, MAGIC, ALU.mult, ALU.add))
            for _ in range(NEWTON):
                steps.link(nc.vector.tensor_tensor(t, y, y, ALU.mult))
                steps.link(nc.vector.tensor_tensor(t, t, v, ALU.mult))
                steps.link(nc.vector.tensor_scalar(t, t, -0.5, 1.5, ALU.mult, ALU.add))
                steps.link(nc.vector.tensor_tensor(y, y, t, ALU.mult))

        def layernorm_coefficients(n, k, d, dis, st, small, scale, shift):
            total, diff, var, room = (small[0:n, m, 0:k] for m in range(4))
            scale, shift, even, odd = scale[0:n, 0:k], shift[0:n, 0:k], st[0:n, 0:k, 0:3], st[0:n, 0:k, 3:6]
            nc.vector.tensor_tensor(total, even[:, :, 1], odd[:, :, 1], ALU.add)
            nc.vector.tensor_tensor(var, even[:, :, 2], odd[:, :, 2], ALU.add)
            if d is not None:
                nc.vector.tensor_scalar(room, d, EPS, None, ALU.mult)
            steps.link(nc.vector.tensor_tensor(diff, even[:, :, 1], odd[:, :, 1], ALU.subtract))
            if d is None:
                nc.vector.tensor_scalar(var, var, 1.0 / D, EPS, ALU.mult, ALU.add)
            else:
                nc.vector.scalar_tensor_tensor(out=var, in0=var, scalar=1.0 / D, in1=room, op0=ALU.mult, op1=ALU.add)
            steps.link(nc.vector.tensor_tensor(diff, diff, diff, ALU.mult))
            steps.link(nc.vector.scalar_tensor_tensor(out=var, in0=diff, scalar=0.25, in1=var,
                                                      op0=ALU.mult, op1=ALU.add))
            rsqrt(scale, var, room)
            if dis is not None:
                steps.link(nc.vector.tensor_tensor(scale, scale, dis, ALU.mult))
            return nc.vector.scalar_tensor_tensor(out=shift, in0=total, scalar=-0.5, in1=scale,
                                                  op0=ALU.mult, op1=ALU.mult)

        with ExitStack() as ph:
            hot_q = ph.enter_context(nc.sbuf_tensor("hot_q", [P, K, P], BF16))
            hot_r = ph.enter_context(nc.sbuf_tensor("hot_r", [P, K, T + 1], BF16))
            iota_q = ph.enter_context(nc.sbuf_tensor("iota_q", [P, P], F16))
            iota_r = ph.enter_context(nc.sbuf_tensor("iota_r", [P, T + 1], F16))
            q = ph.enter_context(nc.sbuf_tensor("q", [P, T + 1], F32))
            r = ph.enter_context(nc.sbuf_tensor("r", [P, T + 1], F32))
            t1 = ph.enter_context(nc.sbuf_tensor("t1", [P, T + 1], F32))
            i1 = ph.enter_context(nc.sbuf_tensor("i1", [P, T + 1], I32))
            rest, term = (ph.enter_context(nc.sbuf_tensor(n, [3 * Q, D], F32)) for n in ("rest", "term"))
            qr = ph.enter_context(nc.sbuf_tensor("qr", [P, 2, K], F32))
            deg = ph.enter_context(nc.psum_tensor("deg", [P, 512], F32))
            edges_in, weights_in = ph.enter_context(nc.semaphore("edges_in")), sem("weights_in")
            pads_set, consts_set = ph.enter_context(nc.semaphore("pads_set")), sem("consts_set")
            rows_set = ph.enter_context(nc.semaphore("rows_set"))
            hots_ready = ph.enter_context(nc.semaphore("hots_ready"))
            hots_used = ph.enter_context(nc.semaphore("hots_used"))
            block = ph.enter_context(nc.Block())
            PADS, CONSTS = 3, 9

            @block.sync
            def _(sp):
                sp.wait_ge(pads_set, PADS)
                for held, edges in ((src_i, src), (dst_i, dst), (ew, edge_weight)):
                    sp.dma_start(held[:, 0:T], edges[0:main].rearrange("(p t) -> p t", t=T)).then_inc(edges_in, 16)
                    sp.dma_start(held[0:TAIL, T:T + 1], edges[main:N].rearrange("(p t) -> p t", t=1)).then_inc(edges_in, 16)
                for held, w in ((w1e, we1), (w2e, we2), (w1n, wn1), (w2n, wn2)):
                    sp.dma_start(held[:, :], w[:, :]).then_inc(weights_in, 16)
                for held, b in ((b1e, be1), (b1n, bn1)):
                    sp.dma_start(held[:, :], b.rearrange("(p t) -> p t", t=1)).then_inc(weights_in, 16)
                for held, b in ((b2e, be2), (b2n, bn2)):
                    sp.dma_start(held[:, :], b.partition_broadcast(3 * Q)).then_inc(weights_in, 16)
                sp.wait_ge(weights_in, 16 * 8)

            @block.gpsimd
            def _(pool):
                for held in (src_i, dst_i, ew):
                    nc.gpsimd.memset(held[:, T:T + 1], 0).then_inc(pads_set, 1)
                nc.gpsimd.iota(iota_q[:, :], [[1, P]], base=0, channel_multiplier=0,
                               allow_small_or_imprecise_dtypes=True).then_inc(consts_set, 1)
                nc.gpsimd.iota(iota_r[:, :], [[1, T + 1]], base=0, channel_multiplier=0,
                               allow_small_or_imprecise_dtypes=True).then_inc(consts_set, 1)
                nc.gpsimd.iota(spare_row[:, :], [[0, 1]], base=N, channel_multiplier=1,
                               allow_small_or_imprecise_dtypes=True).then_inc(consts_set, 1)
                nc.gpsimd.memset(zeros[:, :], 0.0).then_inc(consts_set, 1)
                nc.gpsimd.memset(before[:, :], 1.0).then_inc(consts_set, 1)
                nc.gpsimd.memset(ident[:, :], 0.0).then_inc(consts_set, 1)
                pool.wait_ge(consts_set, 6)
                nc.gpsimd.affine_select(out=ident[:, :], in_=ident[:, :], compare_op=ALU.not_equal, fill=1.0, base=0,
                                        pattern=[[-1, P]], channel_multiplier=1).then_inc(consts_set, 1)
                for at in (0, 2 * P):
                    nc.gpsimd.affine_select(out=before[:, at:at + P], in_=before[:, at:at + P], compare_op=ALU.is_gt,
                                            fill=0.0, base=0, pattern=[[-1, P]],
                                            channel_multiplier=1).then_inc(consts_set, 1)

            @block.vector
            def _(dve):
                steps.eng = dve
                steps.link(nc.vector.memset(first_rows[:, :], 0.0))
                for at in range(0, 3 * Q, Q):
                    nc.vector.memset(first_rows[at:at + 1, :], 1.0).then_inc(rows_set, 1)
                dve.wait_ge(edges_in, 16 * 6)
                nc.vector.tensor_copy(src_f[:, :], src_i[:, :])
                steps.link(nc.vector.tensor_copy(dst_f[:, :], dst_i[:, :]))
                steps.link(nc.vector.tensor_scalar(i1[:, :], src_f[:, :], 1.0 / T, None, ALU.mult))
                steps.link(nc.vector.tensor_copy(q[:, :], i1[:, :]))
                steps.link(nc.vector.scalar_tensor_tensor(out=r[:, :], in0=q[:, :], scalar=-float(T), in1=src_f[:, :],
                                                          op0=ALU.mult, op1=ALU.add))
                for op, bound, sign in ((ALU.is_lt, 0.0, -1.0), (ALU.is_ge, float(T), 1.0)):
                    steps.link(nc.vector.tensor_scalar(t1[:, :], r[:, :], bound, sign, op, ALU.mult))
                    nc.vector.tensor_tensor(q[:, :], q[:, :], t1[:, :], ALU.add)
                    steps.link(nc.vector.scalar_tensor_tensor(out=r[:, :], in0=t1[:, :], scalar=-float(T),
                                                              in1=r[:, :], op0=ALU.mult, op1=ALU.add))
                steps.link(nc.vector.tensor_scalar(t1[:, :], src_f[:, :], float(main), None, ALU.is_ge))
                steps.link(nc.vector.scalar_tensor_tensor(out=d_all[:, :], in0=r[:, :], scalar=-float(P), in1=t1[:, :],
                                                          op0=ALU.add, op1=ALU.mult))
                steps.link(nc.vector.tensor_tensor(q[:, :], q[:, :], d_all[:, :], ALU.add))
                steps.link(nc.vector.scalar_tensor_tensor(out=d_all[:, :], in0=r[:, :], scalar=-float(T), in1=t1[:, :],
                                                          op0=ALU.add, op1=ALU.mult))
                steps.link(nc.vector.tensor_tensor(r[:, :], r[:, :], d_all[:, :], ALU.subtract))
                dve.wait_ge(consts_set, CONSTS)

                def hots(tiles, n, at_q, at_r):
                    for j in tiles:
                        nc.vector.tensor_scalar(hot_q[0:n, j, :], iota_q[0:n, :], at_q[0:n, j:j + 1], None,
                                                ALU.is_equal)
                        last = nc.vector.tensor_scalar(hot_r[0:n, j, :], iota_r[0:n, :], at_r[0:n, j:j + 1],
                                                       None, ALU.is_equal)
                    last.then_inc(hots_ready, 1)

                with dve.Fori(0, NG) as g:
                    steps.enter(g, 2)
                    for half in range(2):
                        dve.wait_ge(hots_used, g * 2 + (half + 1))
                        at, now = slice(half * K // 2, (half + 1) * K // 2), bass.ds(g * K + half * K // 2, K // 2)
                        nc.vector.tensor_copy(qr[:, 0, at], q[:, now])
                        steps.link(nc.vector.tensor_copy(qr[:, 1, at], r[:, now]))
                        hots(range(half * K // 2, (half + 1) * K // 2), P, qr[:, 0, :], qr[:, 1, :])
                steps.leave(NG)
                dve.wait_ge(hots_used, NG * 2 + 1)
                hots([0], TAIL, q[:, T:T + 1], r[:, T:T + 1])

                dve.wait_ge(weights_in, 16 * 8)
                for b2, terms in ((b2e, b2e_terms), (b2n, b2n_terms)):
                    steps.link(nc.vector.tensor_copy(rest[:, :], b2[:, :]))
                    for quadrant in range(3):
                        steps.link(nc.vector.tensor_copy(terms[:, 0:D], rest[:, :]))
                        if quadrant < 2:
                            for at in range(quadrant + 1, 3):
                                later = slice(at * Q, (at + 1) * Q)
                                steps.link(nc.vector.tensor_copy(term[later, :], terms[later, 0:D]))
                                steps.link(nc.vector.tensor_tensor(rest[later, :], rest[later, :], term[later, :],
                                                                   ALU.subtract))
                    for c in range(1, C):
                        nc.vector.tensor_copy(terms[:, c * D:(c + 1) * D], terms[:, 0:D])
                steps.link(nc.vector.tensor_tensor(t1[:, :], src_f[:, :], dst_f[:, :], ALU.not_equal))
                steps.link(nc.vector.tensor_tensor(ew[:, :], ew[:, :], t1[:, :], ALU.mult))
                dve.wait_ge(hots_used, NG * 2 + 3)
                nc.vector.tensor_scalar(t1[:, :], deg[:, 0:T + 1], 1.0, None, ALU.min)
                steps.link(nc.vector.tensor_scalar(d_all[:, :], deg[:, 0:T + 1], 1.0, None, ALU.max))
                rsqrt(r_all[:, :], d_all[:, :], q[:, :])
                nc.vector.tensor_tensor(s_all[:, :], d_all[:, :], r_all[:, :], ALU.mult)
                steps.link(nc.vector.tensor_tensor(dis_all[:, :], t1[:, :], r_all[:, :], ALU.mult))

            @block.tensor
            def _(pe):
                pe.wait_ge(consts_set, CONSTS)
                pe.wait_ge(rows_set, 3)
                nc.tensor.matmul(deg[:, 0:T + 1], first_rows[:, :],
                                 zeros[0:3 * Q, 0:T + 1].bitcast(BF16)[:, 0:T + 1],
                                 start=True, stop=False, skip_group_check=True)

                pe.sem_inc(hots_used, 2)

                def count(tiles, n, last_of_all=False):
                    for j in tiles:
                        last = nc.tensor.matmul(deg[:, 0:T + 1], hot_q[0:n, j, :], hot_r[0:n, j, :],
                                                start=False, stop=last_of_all, skip_group_check=True)
                    last.then_inc(hots_used, 1)

                with pe.Fori(0, NG) as g:
                    for half in range(2):
                        pe.wait_ge(hots_ready, g * 2 + (half + 1))
                        count(range(half * K // 2, (half + 1) * K // 2), P)
                pe.wait_ge(hots_ready, NG * 2 + 1)
                count([0], TAIL, last_of_all=True)

        def node_groups(eng, group):
            with eng.Fori(0, NGN // 3) as i:
                for b in range(3):
                    group(i * 3 + b, i, b, KN, P)
            group(NGN - 1, NGN // 3, 0, KN, P)
            group(NGN, NGN // 3, 1, 1, TAIL)

        def node_group_after(g, i, b):
            tiles, n = (1, TAIL) if isinstance(g, int) and g == NGN - 1 else (KN, P)
            return g + 1, i + b // 2, (b + 1) % 3, tiles, n

        def node_rows(table, g, tiles):
            if tiles == 1:
                return table[main:N, :].rearrange("(t p) d -> p t d", t=1)
            return rows(table)[:, bass.ds(g * KN, KN), :]

        with ExitStack() as ph:
            def buf(name, shape, dt=F32):
                return ph.enter_context(nc.sbuf_tensor(name, shape, dt))

            def flag(name):
                return ph.enter_context(nc.semaphore(name))

            xt, gt, zt = buf("xt", [P, 3, KN, D]), buf("gt", [P, 3, KN, D]), buf("zt", [P, 3, KN, ZW])
            st, small, coef = buf("st2", [P, KN, 6]), buf("small2", [P, 4, KN]), buf("coef2", [P, 3, 2, KN])
            s_now = buf("s_now", [P, KN])
            x_in = [flag(f"x_in{b}") for b in range(3)]
            coef_ready, g_ready = flag("coef_ready2"), flag("g_ready")
            z_ready = flag("z_ready")
            stored = [flag(f"stored{b}") for b in range(3)]
            block = ph.enter_context(nc.Block())

            @block.sync
            def _(sp):
                def group(g, i, b, tiles, n):
                    sp.wait_ge(z_ready, g + 1)
                    sp.dma_start(xt[0:n, b, 0:tiles, :], node_rows(x, g, tiles)).then_inc(x_in[b], 16)

                node_groups(sp, group)

            @block.vector
            def _(dve):
                steps.eng = dve
                dve.sem_inc(z_ready, 3)
                for b in range(3):
                    last = nc.vector.memset(zt[:, b, :, D + 1:ZW], 0.0)
                steps.link(last)

                def coefficients(g, i, b, tiles, n):
                    dve.wait_ge(x_in[b], i * 16 + 16)
                    for j in range(tiles):
                        last = nc.vector.bn_stats(st[0:n, j, :], xt[0:n, b, j, :])
                    steps.link(last)
                    layernorm_coefficients(n, tiles, None, dis_all[0:n, bass.ds(g * KN, tiles)], st, small,
                                           coef[:, b, 0, :], coef[:, b, 1, :]).then_inc(coef_ready, 1)

                def group(g, i, b, tiles, n):
                    if tiles == KN:
                        coefficients(*node_group_after(g, i, b))
                    dve.wait_ge(stored[b], i * 32 + 16)
                    dve.wait_ge(z_ready, g + 3)
                    nc.vector.tensor_copy(zt[0:n, b, 0:tiles, D], d_all[0:n, bass.ds(g * KN, tiles)])
                    steps.link(nc.vector.tensor_copy(s_now[0:n, 0:tiles], s_all[0:n, bass.ds(g * KN, tiles)]))
                    dve.wait_ge(g_ready, g + 1)
                    for j in range(tiles):
                        last = nc.vector.scalar_tensor_tensor(
                            out=zt[0:n, b, j, 0:D], in0=xt[0:n, b, j, :], scalar=s_now[0:n, j:j + 1],
                            in1=gt[0:n, b, j, :], op0=ALU.mult, op1=ALU.add)
                    last.then_inc(z_ready, 1)

                coefficients(0, 0, 0, KN, P)
                with dve.Fori(0, NGN // 3) as i:
                    steps.enter(i, 3 * (LN_STEPS + 2))
                    for b in range(3):
                        group(i * 3 + b, i, b, KN, P)
                steps.leave(NGN // 3)
                group(NGN - 1, NGN // 3, 0, KN, P)
                group(NGN, NGN // 3, 1, 1, TAIL)

            @block.scalar
            def _(act):
                def group(g, i, b, tiles, n):
                    act.wait_ge(coef_ready, g + 1)
                    act.wait_ge(stored[b], i * 32 + 16)
                    for j in range(tiles):
                        last = nc.scalar.activation(gt[0:n, b, j, :], xt[0:n, b, j, :], ACT.Relu,
                                                    scale=coef[0:n, b, 0, j:j + 1], bias=coef[0:n, b, 1, j:j + 1])
                    last.then_inc(g_ready, 1)

                node_groups(act, group)

            @block.gpsimd
            def _(pool):
                pool.dma_start(z_table[N:N + P // 2, :], zeros[0:P // 2, 0:ZW]).then_inc(stored[0], 16)
                pool.dma_start(z_table[N + P // 2:N + P, :], zeros[0:P // 2, 0:ZW]).then_inc(stored[1], 16)
                pool.dma_start(m_table[main:N, :], zeros[0:TAIL, 0:D]).then_inc(stored[2], 16)

                def group(g, i, b, tiles, n):
                    pool.wait_ge(z_ready, g + 4)
                    pool.dma_start(node_rows(g_table, g, tiles), gt[0:n, b, 0:tiles, :]).then_inc(stored[b], 16)
                    pool.dma_start(node_rows(z_table[0:N, :], g, tiles), zt[0:n, b, 0:tiles, :]).then_inc(stored[b], 16)

                node_groups(pool, group)
                for b in range(3):
                    pool.wait_ge(stored[b], 16 + 32 * len(range(b, NGN + 1, 3)))

        def edge_layer(layer):
            mlp = layer == 2
            table, width, gather_i = (z_table, ZW, src_i) if mlp else (g_table, D, dst_i)
            key_f, keys_by_tile = (dst_f, dst_by_tile) if mlp else (src_f, src_by_tile)
            sums_table, sum_width = (m_table, D) if mlp else (z_table, ZW)
            with ExitStack() as ph:
                def buf(name, shape, dt=F32):
                    return ph.enter_context(nc.sbuf_tensor(f"{name}_{layer}", shape, dt))

                def bank(name):
                    return ph.enter_context(nc.psum_tensor(f"{name}_{layer}", [P, 2 * P], F32))

                def flag(name):
                    return ph.enter_context(nc.semaphore(f"{name}_{layer}"))

                got = buf("got", [P, 2, K, width])
                sums = buf("sums", [P, 2, K, sum_width])
                spread = buf("spread", [P, 2, K * P], I32)
                same = buf("same", [P, 2, PAIRS, 3 * P])
                dup = buf("dup", [P, K])
                junk = buf("junk", [P, 2, 3 * P], BF16)
                gather_at, sums_at = buf("gather_at", [P, 2, K], I32), buf("sums_at", [P, 2, K], I32)
                key, weight = buf("key", [P, 2, K]), buf("weight", [P, 2, K])
                detour = buf("detour", [P, K])
                pair_sums = [bank(f"pair_sums{b}") for b in range(2)]
                indices_staged = flag("indices_staged")
                spread_in = [flag(f"spread_in{b}") for b in range(2)]
                gathered = [flag(f"gathered{b}") for b in range(2)]
                compared = flag("compared")
                rows_picked = flag("rows_picked")
                summed = flag("summed")
                sums_ready = flag("sums_ready")
                sums_added = flag("sums_added")
                added = flag("added")
                waited = flag("waited")
                if mlp:
                    ea = buf("ea", [DE, 2, K * P])
                    hidden = buf("hidden", [P, 2, 2 * P])
                    normed = buf("normed", [P, 2, K, D])
                    message = buf("message", [P, 2, 2, D])
                    st, small, coef = buf("st", [P, K, 6]), buf("small", [P, 4, K]), buf("coef", [P, 2, 2, K])
                    d_now = buf("d_now", [P, K])
                    hidden_p = [bank(f"hidden_p{b}") for b in range(2)]
                    filter_p = [bank(f"filter_p{b}") for b in range(2)]
                    ea_in = [flag(f"ea_in{b}") for b in range(2)]
                    hid_summed = flag("hid_summed")
                    hid_ready = flag("hid_ready")
                    filter_ready, message_ready = flag("filter_ready"), flag("message_ready")
                    coef_ready, normed_ready = flag("coef_ready"), flag("normed_ready")
                else:
                    cleared, fill_set = flag("cleared"), flag("fill_set")
                block = ph.enter_context(nc.Block())

                def pairs(tiles):
                    return [range(j, min(j + 2, tiles)) for j in range(0, tiles, 2)]

                def groups(eng, group, per_turn=None):
                    with eng.Fori(0, NG // 2 - 1) as i:
                        if per_turn is not None:
                            steps.enter(i, per_turn)
                        for b in range(2):
                            group(i * 2 + b, i, b, K, P)
                    if per_turn is not None:
                        steps.leave(NG // 2 - 1)
                    for g in range(NG - 3, NG + 1):
                        group(g, g // 2, g % 2, *size(g))

                def size(g):
                    if isinstance(g, int) and g >= NG:
                        return (1, TAIL) if g == NG else (0, 0)
                    return K, P

                def pair_ahead(g, i, b, k, m):
                    g, i, b, k = (g + 1, i + b, 1 - b, k + m - PAIRS) if k + m >= PAIRS else (g, i, b, k + m)
                    tiles, n = size(g)
                    return (g * PAIRS + k, g, i, b, k, pairs(tiles)[k], n) if k < len(pairs(tiles)) else None

                @block.sync
                def _(sp):
                    def group(g, i, b, tiles, n):
                        at = bass.ds(g * (K * P), tiles * n)
                        sp.wait_ge(compared, g * PAIRS + 1)
                        sp.dma_start(spread[:, b, 0:tiles * n],
                                     keys_by_tile[at].partition_broadcast(P)).then_inc(spread_in[b], 16)
                        if mlp:
                            sp.wait_ge(hid_summed, g * PAIRS + 1)
                            sp.dma_start(ea[:, b, 0:tiles * n], attr_t[:, at]).then_inc(ea_in[b], 16)
                        elif tiles == K:
                            sp.dma_start(rows(m_table)[:, bass.ds(g * K, K), :],
                                         zeros[:, :].rearrange("p (k d) -> p k d", d=D)).then_inc(cleared, 16)

                    groups(sp, group)
                    if not mlp:
                        sp.wait_ge(cleared, 16 * NG)

                @block.gpsimd
                def _(pool):
                    pool.sem_inc(added, K - 1)
                    at = N + (P // 2 if mlp else 0)
                    pool.dma_start(m_table[at:at + P // 2, :], zeros[0:P // 2, 0:D]).then_inc(sums_added, 16)

                    def gather(b, j, n):
                        pool.indirect_dma_start(got[0:n, b, j, :], None, table[:, :],
                                                bass.IndirectOffsetOnAxis(gather_at[0:n, b, j:j + 1], axis=0)
                                                ).then_inc(gathered[b], 16)

                    def group(g, i, b, tiles, n):
                        ahead, ahead_n = size(g + 2)
                        for k, pair in enumerate(pairs(tiles)):
                            if k == 0 and ahead:
                                pool.wait_ge(indices_staged, g + 3)
                                if mlp:
                                    pool.wait_ge(normed_ready, g + 1)
                                else:
                                    pool.wait_ge(summed, g * PAIRS + (2 * PAIRS + 1))
                                pool.sem_inc(waited, 1)
                            for j in pair:
                                if j < ahead:
                                    gather(b, j, ahead_n)
                            pool.wait_ge(sums_added, (g * PAIRS + k) * 32 + 16)
                            pool.sem_inc(added, 1)
                            if k == 0:
                                pool.wait_ge(rows_picked, g + 1)
                            pool.wait_ge(sums_ready, g * PAIRS + (k + 3))
                            pool.sem_inc(waited, 1)
                            for j in pair:
                                pool.indirect_dma_start(
                                    sums_table[:, :], bass.IndirectOffsetOnAxis(sums_at[0:n, b, j:j + 1], axis=0),
                                    sums[0:n, b, j, :], None, compute_op=ALU.add).then_inc(sums_added, 16)

                    for g in range(2):
                        pool.wait_ge(indices_staged, g + 1)
                        for j in range(K):
                            gather(g, j, P)
                    groups(pool, group)
                    pool.wait_ge(sums_added, 16 * (T + 2))

                @block.vector
                def _(dve):
                    steps.eng = dve
                    dve.sem_inc(compared, PAIRS + 1)
                    if mlp:
                        dve.sem_inc(message_ready, 2)

                    def stage_indices(g, b, tiles, n):
                        nc.vector.tensor_copy(gather_at[0:n, b, 0:tiles],
                                              gather_i[0:n, bass.ds(g * K, tiles)]).then_inc(indices_staged, 1)

                    def stage_keys(g, i, b, tiles, n):
                        cols = bass.ds(g * K, tiles)
                        if not mlp:
                            nc.vector.tensor_copy(weight[0:n, b, 0:tiles], ew[0:n, cols])
                        steps.link(nc.vector.tensor_copy(key[0:n, b, 0:tiles], key_f[0:n, cols]))
                        dve.wait_ge(spread_in[b], i * 16 + 16)
                        dve.wait_ge(summed, g * PAIRS + 1)

                    def compare(g, b, k, tiles, n):
                        dve.wait_ge(compared, g * PAIRS + (k + PAIRS))
                        for m, j in enumerate(pairs(tiles)[k]):
                            others = n if tiles == 1 else (m + 1) * P
                            at = m * P
                            mine, theirs = key[0:n, b, j:j + 1], spread[0:n, b, 2 * k * P:2 * k * P + others]
                            if mlp:
                                nc.vector.tensor_scalar(same[0:n, b, k, at:at + others], theirs, mine, None,
                                                        ALU.is_equal)
                            else:
                                nc.vector.tensor_scalar(same[0:n, b, k, at:at + others], theirs, mine,
                                                        weight[0:n, b, j:j + 1], ALU.is_equal, ALU.mult)
                            last = nc.vector.scalar_tensor_tensor(
                                out=junk[0:n, (b + k) % 2, at:at + others], in0=theirs, scalar=mine,
                                in1=before[0:n, at:at + others], op0=ALU.is_equal, op1=ALU.mult,
                                accum_out=dup[0:n, j:j + 1])
                        last.then_inc(compared, 1)

                    def pick_rows(g, b, tiles, n):
                        dve.wait_ge(compared, g * PAIRS + (len(pairs(tiles)) + PAIRS + 1))
                        mine, many, way = key[0:n, b, 0:tiles], dup[0:n, 0:tiles], detour[0:n, 0:tiles]
                        steps.link(nc.vector.tensor_scalar(way, mine, -1.0, spare_row[0:n, :], ALU.mult, ALU.add))
                        steps.link(nc.vector.scalar_tensor_tensor(out=way, in0=many, scalar=1.0, in1=way,
                                                                  op0=ALU.min, op1=ALU.mult))
                        dve.wait_ge(added, g * PAIRS + PAIRS)
                        nc.vector.tensor_tensor(sums_at[0:n, b, 0:tiles], mine, way, ALU.add).then_inc(rows_picked, 1)

                    def norm(g, i, b, tiles, n):
                        dve.wait_ge(gathered[b], i * 16 * K + 16 * tiles)
                        nc.vector.tensor_copy(d_now[0:n, 0:tiles], got[0:n, b, 0:tiles, D])
                        for j in range(tiles):
                            last = nc.vector.bn_stats(st[0:n, j, :], got[0:n, b, j, 0:D])
                        steps.link(last)
                        layernorm_coefficients(n, tiles, d_now[0:n, 0:tiles], None, st, small,
                                               coef[:, b, 0, :], coef[:, b, 1, :]).then_inc(coef_ready, 1)

                    def send(g, b, k, pair, n):
                        p = g * PAIRS + k
                        if k == 0:
                            dve.wait_ge(normed_ready, g + 1)
                        dve.wait_ge(filter_ready, p + 3)
                        dve.wait_ge(summed, p + PAIRS)
                        nc.vector.tensor_tensor(
                            message[0:n, (b + k) % 2, 0:len(pair), :], normed[0:n, b, pair[0]:pair[-1] + 1, :],
                            filter_p[(b + k) % 2][0:n, 0:len(pair) * D].rearrange("p (j d) -> p j d", d=D),
                            ALU.mult).then_inc(message_ready, 1)

                    def group(g, i, b, tiles, n):
                        nxt, nxt_n = size(g + 1)
                        if size(g + 2)[0]:
                            if not mlp:
                                dve.wait_ge(gathered[b], i * 16 * K + 16 * K)
                            stage_indices(g + 2, b, *size(g + 2))
                        if nxt:
                            dve.wait_ge(rows_picked, g + 1)
                            stage_keys(g + 1, i + b, 1 - b, nxt, nxt_n)
                        for k in range(PAIRS):
                            if mlp and k < len(pairs(tiles)):
                                send(g, b, k, pairs(tiles)[k], n)
                            if k < len(pairs(nxt)):
                                compare(g + 1, 1 - b, k, nxt, nxt_n)
                            if mlp and nxt and k == 2:
                                norm(g + 1, i + b, 1 - b, nxt, nxt_n)
                        if nxt:
                            pick_rows(g + 1, 1 - b, nxt, nxt_n)

                    for g in range(2):
                        stage_indices(g, g, K, P)
                    stage_keys(0, 0, 0, K, P)
                    for k in range(PAIRS):
                        compare(0, 0, k, K, P)
                    pick_rows(0, 0, K, P)
                    if mlp:
                        norm(0, 0, 0, K, P)
                    groups(dve, group, 2 * (3 + (LN_STEPS if mlp else 0)))

                @block.scalar
                def _(act):
                    act.sem_inc(sums_ready, 2)
                    if mlp:
                        act.sem_inc(hid_ready, 2)
                    else:
                        for b in range(2):
                            nc.scalar.activation(sums[:, b, :, D:ZW], zeros[:, 0:K * (ZW - D)].rearrange(
                                "p (k d) -> p k d", k=K), ACT.Copy).then_inc(fill_set, 1)
                        act.wait_ge(fill_set, 2)

                    def norm(g, b, tiles, n):
                        act.wait_ge(coef_ready, g + 1)
                        for j in range(tiles):
                            last = nc.scalar.activation(
                                normed[0:n, b, j, :], got[0:n, b, j, 0:D], ACT.Relu,
                                scale=coef[0:n, b, 0, j:j + 1], bias=coef[0:n, b, 1, j:j + 1])
                        last.then_inc(normed_ready, 1)

                    def hide(p, g, i, b, k, pair, n):
                        act.wait_ge(hid_summed, p + (PAIRS + 2))
                        act.wait_ge(filter_ready, p + 1)
                        nc.scalar.activation(hidden[:, (b + k) % 2, 0:len(pair) * n],
                                             hidden_p[(b + k) % 2][:, 0:len(pair) * n], ACT.Silu,
                                             bias=b1e[:, 0:1]).then_inc(hid_ready, 1)

                    def group(g, i, b, tiles, n):
                        for k, pair in enumerate(pairs(tiles)):
                            p = g * PAIRS + k
                            if mlp and (to := pair_ahead(g, i, b, k, 2)):
                                hide(*to)
                            act.wait_ge(summed, p + (PAIRS + 2))
                            act.wait_ge(added, p + 1)
                            nc.scalar.activation(
                                sums[0:n, b, pair[0]:pair[-1] + 1, 0:D],
                                pair_sums[(b + k) % 2][0:n, 0:len(pair) * D].rearrange("p (j d) -> p j d", d=D),
                                ACT.Copy).then_inc(sums_ready, 1)
                            if mlp and k == 3 and size(g + 1)[0]:
                                norm(g + 1, 1 - b, *size(g + 1))

                    if mlp:
                        hide(*pair_ahead(0, 0, 0, 0, 0))
                        hide(*pair_ahead(0, 0, 0, 0, 1))
                        norm(0, 0, K, P)
                    groups(act, group)

                @block.tensor
                def _(pe):
                    pe.sem_inc(summed, PAIRS + 1)
                    if mlp:
                        pe.sem_inc(hid_summed, PAIRS + 1)
                        pe.sem_inc(filter_ready, 2)

                    def hide(p, g, i, b, k, pair, n):
                        if k == 0:
                            pe.wait_ge(ea_in[b], i * 16 + 16)
                        pe.wait_ge(hid_ready, p + 1)
                        cols = len(pair) * n
                        nc.tensor.matmul(hidden_p[(b + k) % 2][:, 0:cols], w1e[:, :],
                                         ea[:, b, 2 * k * P:2 * k * P + cols],
                                         start=True, stop=True).then_inc(hid_summed, 1)

                    def make_filter(p, g, i, b, k, pair, n):
                        bank_ = filter_p[(b + k) % 2]
                        pe.wait_ge(message_ready, p + 1)
                        nc.tensor.matmul(bank_[0:n, 0:len(pair) * D], first_rows[:, 0:n], b2e_terms[:, 0:len(pair) * D],
                                         start=True, stop=False, skip_group_check=True)
                        pe.wait_ge(hid_ready, p + 3)
                        for m in range(len(pair)):
                            last = nc.tensor.matmul(bank_[0:n, m * D:(m + 1) * D],
                                                    hidden[:, (b + k) % 2, m * n:(m + 1) * n], w2e[:, :],
                                                    start=False, stop=(m == len(pair) - 1), skip_group_check=True)
                        last.then_inc(filter_ready, 1)

                    def group(g, i, b, tiles, n):
                        for k, pair in enumerate(pairs(tiles)):
                            p = g * PAIRS + k
                            if mlp:
                                if to := pair_ahead(g, i, b, k, 2):
                                    hide(*to)
                                if to := pair_ahead(g, i, b, k, 1):
                                    make_filter(*to)
                                pe.wait_ge(message_ready, p + 3)
                                data = [message[0:n, (b + k) % 2, m, :] for m in range(len(pair))]
                            else:
                                if k == 0:
                                    pe.wait_ge(gathered[b], i * 16 * K + 16 * tiles)
                                data = [got[0:n, b, j, :] for j in pair]
                            pe.wait_ge(compared, p + (PAIRS + 2))
                            pe.wait_ge(sums_ready, p + 1)
                            bank_, same_ = pair_sums[(b + k) % 2], same[0:n, b, k, :]
                            last = nc.tensor.matmul(bank_[0:n, 0:D], same_[:, 0:n], data[0],
                                                    start=True, stop=(len(pair) == 1))
                            if len(pair) == 2:
                                nc.tensor.matmul(bank_[:, 0:D], same_[:, P:2 * P], data[1], start=False, stop=True)
                                last = nc.tensor.matmul(bank_[:, D:2 * D], same_[:, 2 * P:3 * P], data[1],
                                                        start=True, stop=True)
                            last.then_inc(summed, 1)

                    if mlp:
                        hide(*pair_ahead(0, 0, 0, 0, 0))
                        hide(*pair_ahead(0, 0, 0, 0, 1))
                        make_filter(*pair_ahead(0, 0, 0, 0, 0))
                    groups(pe, group)

        edge_layer(1)
        edge_layer(2)

        with ExitStack() as ph:
            def buf(name, shape, dt=F32):
                return ph.enter_context(nc.sbuf_tensor(name, shape, dt))

            def flag(name):
                return ph.enter_context(nc.semaphore(name))

            def banks(name):
                return [ph.enter_context(nc.psum_tensor(f"{name}{b}", [P, C * P], F32)) for b in range(2)]

            zn, mn = buf("zn", [P, 3, KN, ZW]), buf("mn", [P, 3, KN, D])
            on = buf("on", [P, 3, KN, D])
            st, small, coef = buf("st5", [P, KN, 6]), buf("small5", [P, 4, KN]), buf("coef5", [P, 3, 2, KN])
            r_now = buf("r_now", [P, 3, KN])
            mt, hidden = buf("mt", [P, 2, C * P]), buf("hidden5", [P, 2, C * P])
            mt_p, hidden_p, out_p = banks("mt_p"), banks("hidden5_p"), banks("out_p")
            rows_in = [flag(f"rows_in{b}") for b in range(3)]
            rows_out = [flag(f"rows_out{b}") for b in range(3)]
            coef_ready, h_ready = flag("coef5_ready"), flag("h_ready")
            out_ready = flag("out_ready")
            turned, mt_ready = flag("turned"), flag("mt_ready")
            hid_summed, hid_ready = flag("hid5_summed"), flag("hid5_ready")
            branch_summed, branch_added = flag("branch_summed"), flag("branch_added")
            block = ph.enter_context(nc.Block())
            CH = KN // C
            HALF = CH // 2

            def chunks(tiles):
                return [range(j, min(j + C, tiles)) for j in range(0, tiles, C)]

            def chunk_ahead(g, i, b, k, m):
                if isinstance(g, int) and g == NGN:
                    return None
                if k + m < CH:
                    return g * CH + (k + m), i, b, k + m, chunks(KN)[k + m], P
                g, i, b, tiles, n = node_group_after(g, i, b)
                k = k + m - CH
                return (g * CH + k, i, b, k, chunks(tiles)[k], n) if k < len(chunks(tiles)) else None

            @block.sync
            def _(sp):
                def group(g, i, b, tiles, n):
                    sp.wait_ge(out_ready, g + 1)
                    sp.dma_start(mn[0:n, b, 0:tiles, :], node_rows(m_table[0:N, :], g, tiles)).then_inc(rows_in[b], 16)
                    sp.dma_start(zn[0:n, b, 0:tiles, :], node_rows(z_table[0:N, :], g, tiles)).then_inc(rows_in[b], 16)

                node_groups(sp, group)

            @block.gpsimd
            def _(pool):
                for b in range(3):
                    pool.dma_start(z_table[N + b:N + b + 1, :], zeros[0:1, 0:ZW]).then_inc(rows_out[b], 16)

                def group(g, i, b, tiles, n):
                    pool.wait_ge(out_ready, g + 4)
                    pool.dma_start(node_rows(out, g, tiles), on[0:n, b, 0:tiles, :]).then_inc(rows_out[b], 16)

                node_groups(pool, group)
                for b in range(3):
                    pool.wait_ge(rows_out[b], 16 + 16 * len(range(b, NGN + 1, 3)))

            @block.vector
            def _(dve):
                steps.eng = dve
                dve.sem_inc(out_ready, 3)
                dve.sem_inc(branch_added, 2)

                def stats(i, b, js, n):
                    dve.wait_ge(rows_in[b], i * 32 + 32)
                    for j in js:
                        last = nc.vector.bn_stats(st[0:n, j, :], zn[0:n, b, j, 0:D])
                    return last

                def coefficients(g, i, b, tiles, n):
                    cols = bass.ds(g * KN, tiles)
                    steps.link(nc.vector.tensor_copy(r_now[0:n, b, 0:tiles], r_all[0:n, cols]))
                    layernorm_coefficients(n, tiles, d_all[0:n, cols], None, st, small,
                                           coef[:, b, 0, :], coef[:, b, 1, :]).then_inc(coef_ready, 1)

                def group(g, i, b, tiles, n):
                    nxt = node_group_after(g, i, b) if tiles == KN else None
                    per = KN // HALF

                    def add_x1(k):
                        dve.wait_ge(branch_added, g * CH + (k + 3))
                        for j in chunks(tiles)[k]:
                            last = nc.vector.scalar_tensor_tensor(
                                out=on[0:n, b, j, :], in0=zn[0:n, b, j, 0:D], scalar=r_now[0:n, b, j:j + 1],
                                in1=on[0:n, b, j, :], op0=ALU.mult, op1=ALU.add)
                        return last

                    dve.wait_ge(h_ready, g + 1)
                    for k, js in enumerate(chunks(tiles)):
                        here = on[0:n, b, js[0]:js[-1] + 1, :]
                        dve.wait_ge(branch_summed, g * CH + (k + 3))
                        nc.vector.tensor_tensor(here, out_p[k % 2][0:n, 0:len(js) * D].rearrange("p (j d) -> p j d", d=D),
                                                here, ALU.add).then_inc(branch_added, 1)
                        if k:
                            add_x1(k - 1)
                        if nxt and k < HALF and k * per < nxt[3]:
                            stats(nxt[1], nxt[2], range(k * per, min(k * per + per, nxt[3])), nxt[4])
                        if nxt and k == HALF - 1:
                            coefficients(*nxt)
                    add_x1(len(chunks(tiles)) - 1).then_inc(out_ready, 1)

                stats(0, 0, range(KN), P)
                coefficients(0, 0, 0, KN, P)
                with dve.Fori(0, NGN // 3) as i:
                    steps.enter(i, 3 * LN_STEPS)
                    for b in range(3):
                        group(i * 3 + b, i, b, KN, P)
                steps.leave(NGN // 3)
                group(NGN - 1, NGN // 3, 0, KN, P)
                group(NGN, NGN // 3, 1, 1, TAIL)

            @block.scalar
            def _(act):
                act.sem_inc(hid_ready, 2)

                def norm(b, js, n):
                    for j in js:
                        last = nc.scalar.activation(on[0:n, b, j, :], zn[0:n, b, j, 0:D], ACT.Relu,
                                                    scale=coef[0:n, b, 0, j:j + 1], bias=coef[0:n, b, 1, j:j + 1])
                    return last

                def turn(q, i, b, k, js, n):
                    act.wait_ge(turned, q + 1)
                    act.wait_ge(hid_summed, q + 1)
                    nc.scalar.activation(mt[:, k % 2, 0:len(js) * n], mt_p[k % 2][:, 0:len(js) * n],
                                         ACT.Copy).then_inc(mt_ready, 1)

                def hide(q, i, b, k, js, n):
                    act.wait_ge(hid_summed, q + 3)
                    act.wait_ge(branch_summed, q + 1)
                    nc.scalar.activation(hidden[:, k % 2, 0:len(js) * n], hidden_p[k % 2][:, 0:len(js) * n], ACT.Silu,
                                         bias=b1n[:, 0:1]).then_inc(hid_ready, 1)

                def group(g, i, b, tiles, n):
                    nxt = node_group_after(g, i, b) if tiles == KN else None
                    per = KN // HALF
                    for k in range(len(chunks(tiles))):
                        if to := chunk_ahead(g, i, b, k, 2):
                            turn(*to)
                        if to := chunk_ahead(g, i, b, k, 1):
                            hide(*to)
                        if nxt and k >= HALF:
                            first = (k - HALF) * per
                            if k == HALF:
                                act.wait_ge(coef_ready, g + 2)
                                act.wait_ge(rows_out[nxt[2]], nxt[1] * 16 + 16)
                            if first < nxt[3]:
                                last = norm(nxt[2], range(first, min(first + per, nxt[3])), nxt[4])
                            if first < nxt[3] <= first + per:
                                last.then_inc(h_ready, 1)

                act.wait_ge(coef_ready, 1)
                norm(0, range(KN), P).then_inc(h_ready, 1)
                turn(*chunk_ahead(0, 0, 0, 0, 0))
                turn(*chunk_ahead(0, 0, 0, 0, 1))
                hide(*chunk_ahead(0, 0, 0, 0, 0))
                node_groups(act, group)

            @block.tensor
            def _(pe):
                pe.sem_inc(hid_summed, 2)
                pe.sem_inc(branch_summed, 2)

                def turn(q, i, b, k, js, n):
                    if k == 0:
                        pe.wait_ge(rows_in[b], i * 32 + 32)
                    for m, j in enumerate(js):
                        last = nc.tensor.transpose(mt_p[k % 2][:, m * n:(m + 1) * n], mn[0:n, b, j, :], ident[0:n, 0:n])
                    last.then_inc(turned, 1)

                def hide(q, i, b, k, js, n):
                    pe.wait_ge(mt_ready, q + 1)
                    pe.wait_ge(hid_ready, q + 1)
                    nc.tensor.matmul(hidden_p[k % 2][:, 0:len(js) * n], w1n[:, :], mt[:, k % 2, 0:len(js) * n],
                                     start=True, stop=True).then_inc(hid_summed, 1)

                def group(g, i, b, tiles, n):
                    for k, js in enumerate(chunks(tiles)):
                        q = g * CH + k
                        if to := chunk_ahead(g, i, b, k, 2):
                            turn(*to)
                        if to := chunk_ahead(g, i, b, k, 1):
                            hide(*to)
                        pe.wait_ge(branch_added, q + 1)
                        nc.tensor.matmul(out_p[k % 2][0:n, 0:len(js) * D], first_rows[:, 0:n], b2n_terms[:, 0:len(js) * D],
                                         start=True, stop=False, skip_group_check=True)
                        pe.wait_ge(hid_ready, q + 3)
                        for m in range(len(js)):
                            last = nc.tensor.matmul(out_p[k % 2][0:n, m * D:(m + 1) * D],
                                                    hidden[:, k % 2, m * n:(m + 1) * n], w2n[:, :],
                                                    start=False, stop=(m == len(js) - 1), skip_group_check=True)
                        last.then_inc(branch_summed, 1)

                turn(*chunk_ahead(0, 0, 0, 0, 0))
                turn(*chunk_ahead(0, 0, 0, 0, 1))
                hide(*chunk_ahead(0, 0, 0, 0, 0))
                node_groups(pe, group)


INPUTS = ["x", "src", "dst", "src_by_tile", "dst_by_tile", "attr_t", "edge_weight", "L1_gnn_We1", "L1_gnn_be1",
          "L1_gnn_We2", "L1_gnn_be2", "L1_gnn_Wn1", "L1_gnn_bn1", "L1_gnn_Wn2", "L1_gnn_bn2"]


def kernel(**inputs):
    import numpy as np
    import concourse.bacc as bacc
    from concourse.bass_utils import run_bass_kernel_spmd

    def by_tile(a):
        a = np.asarray(a)
        full = a[:P * T].reshape(P, T, *a.shape[1:]).swapaxes(0, 1)
        return np.concatenate([full.reshape(P * T, *a.shape[1:]), a[P * T:]])

    inputs["src_by_tile"] = by_tile(inputs["src"])
    inputs["dst_by_tile"] = by_tile(inputs["dst"])
    inputs["attr_t"] = by_tile(inputs["edge_attr_50"]).T
    nc = bacc.Bacc("TRN2", target_bir_lowering=False, num_devices=1)
    arrays, args = {}, []
    for name in INPUTS:
        a = np.ascontiguousarray(inputs[name])
        arrays[f"in_{name}"] = a
        args.append(nc.dram_tensor(f"in_{name}", a.shape, mybir.dt.from_np(a.dtype), kind="ExternalInput").ap())
    args.append(nc.dram_tensor("out", (N, D), F32, kind="ExternalOutput").ap())
    build(nc, *args)
    return run_bass_kernel_spmd(nc, [arrays], core_ids=[0]).results[0]["out"]
```

```python
import concourse.bass as bass
from concourse import mybir
from contextlib import ExitStack

ALU = mybir.AluOpType
ACT = mybir.ActivationFunctionType
F32 = mybir.dt.float32
F16 = mybir.dt.float16
BF16 = mybir.dt.bfloat16
I32 = mybir.dt.int32

N = 50000
D = 128
DE = 50
P = 128
Q = 32
T = N // P
TAIL = N - P * T
K = 10
NG = T // K
PAIRS = K // 2
RING = 8
ACT_K = 2
PACE = {1: 3, 2: 1}
ACT_TILES = 8
AHEAD = {1: 4, 2: 6}
ZW = 132
EPS = 1e-5
MAGIC = float(0x5F3759DF)
NEWTON = 3
RSQRT_STEPS = 1 + 4 * NEWTON
assert NG * K == T and NG % 3 == 0 and NG % 2 == 1 and PAIRS > 2
assert ACT_TILES == K - 2 and RING % 2 == 0 and NG % 2 == 1 and 2 < NG % RING < RING
assert max(AHEAD.values()) <= RING - 2


class Steps:

    def __init__(self, sem, waited=None):
        self.eng, self.sem, self.start, self.n, self.waited = None, sem, 0, 0, waited

    def link(self, instruction, scalar=False):
        instruction.then_inc(self.sem, 1)
        self.n += 1
        self.eng.wait_ge(self.sem, self.start + self.n)
        if self.waited and scalar:
            self.eng.sem_inc(self.waited, 1)

    def enter(self, i, per_turn, first=0):
        self.before = self.start + self.n - first * per_turn
        self.start, self.n, self.per_turn = i * per_turn + self.before, 0, per_turn

    def leave(self, turns):
        assert self.n == self.per_turn, (self.n, self.per_turn)
        self.start, self.n = self.before + turns * self.per_turn, 0


def build(nc, x, src, dst, src_by_tile, dst_by_tile, attr_t, edge_weight, we1, be1, we2, be2, wn1, bn1, wn2, bn2, out):
    main = P * T
    with ExitStack() as ctx:
        def sb(name, shape, dt=F32):
            return ctx.enter_context(nc.sbuf_tensor(name, shape, dt))

        def sem(name):
            return ctx.enter_context(nc.semaphore(name))

        g_table = nc.dram_tensor("g_table", (N, D), F32).ap()
        z_table = nc.dram_tensor("z_table", (N + P, ZW), F32).ap()
        m_table = nc.dram_tensor("m_table", (N + P, D), F32).ap()

        def rows(table):
            return table[0:main, :].rearrange("(p t) d -> p t d", t=T)

        src_i, dst_i = sb("src_i", [P, T + 1], I32), sb("dst_i", [P, T + 1], I32)
        src_f, dst_f = sb("src_f", [P, T + 1]), sb("dst_f", [P, T + 1])
        ew = sb("ew", [P, T + 1])
        d_all, r_all, s_all, dis_all = (sb(n, [P, T + 1]) for n in ("d_all", "r_all", "s_all", "dis_all"))
        eps_d_all = sb("eps_d_all", [P, T + 1])
        ident = sb("ident", [P, P])
        before = sb("before", [P, 3 * P])
        spare_row = sb("spare_row", [P, 1])
        zeros = sb("zeros", [P, K * D])
        w1e, w2e, w1n, w2n = sb("w1e", [DE, D]), sb("w2e", [D, D]), sb("w1n", [D, D]), sb("w2n", [D, D])
        b1e, b1n = sb("b1e", [D, 1]), sb("b1n", [D, 1])
        b2e, b2n = sb("b2e", [3 * Q, D]), sb("b2n", [3 * Q, D])
        b2e_terms, b2n_terms = sb("b2e_terms", [3 * Q, 2 * D], BF16), sb("b2n_terms", [3 * Q, 2 * D], BF16)
        first_rows = sb("first_rows", [3 * Q, P], BF16)
        pool_waited = sem("pool_waited")
        steps, pool_steps = Steps(sem("dve_steps")), Steps(sem("pool_steps"), pool_waited)

        def rsqrt(e, steps, y, v, t):
            steps.link(e.tensor_scalar(y.bitcast(I32), v.bitcast(I32), -0.5, MAGIC, ALU.mult, ALU.add))
            for _ in range(NEWTON):
                steps.link(e.tensor_tensor(t, y, y, ALU.mult))
                steps.link(e.tensor_tensor(t, t, v, ALU.mult), scalar=True)
                steps.link(e.tensor_scalar(t, t, -0.5, 1.5, ALU.mult, ALU.add))
                steps.link(e.tensor_tensor(y, y, t, ALU.mult))

        def layernorm_scale(e, steps, n, k, eps_d, st, small, scale):
            total, diff, var, room = (small[0:n, m, 0:k] for m in range(4))
            even, odd = st[0:n, 0:k, 0:3], st[0:n, 0:k, 3:6]
            e.tensor_tensor(total, even[:, :, 1], odd[:, :, 1], ALU.add)
            e.tensor_tensor(var, even[:, :, 2], odd[:, :, 2], ALU.add)
            steps.link(e.tensor_tensor(diff, even[:, :, 1], odd[:, :, 1], ALU.subtract), scalar=True)
            e.tensor_scalar(var, var, 1.0 / D, EPS if eps_d is None else 0.0, ALU.mult, ALU.add)
            e.tensor_scalar(total, total, -0.5, 0.0, ALU.mult, ALU.add)
            steps.link(e.tensor_tensor(diff, diff, diff, ALU.mult), scalar=True)
            steps.link(e.tensor_scalar(diff, diff, 0.25, 0.0, ALU.mult, ALU.add))
            if eps_d is not None:
                steps.link(e.tensor_tensor(var, var, eps_d, ALU.add))
            steps.link(e.tensor_tensor(var, var, diff, ALU.add), scalar=True)
            rsqrt(e, steps, scale[0:n, 0:k], var, room)

        def layernorm_shift(e, steps, n, k, dis, small, scale, shift):
            scale, shift = scale[0:n, 0:k], shift[0:n, 0:k]
            if dis is not None:
                steps.link(e.tensor_tensor(scale, scale, dis, ALU.mult))
            return e.tensor_tensor(shift, small[0:n, 0, 0:k], scale, ALU.mult)

        def layernorm_coefficients(e, steps, n, k, eps_d, dis, st, small, scale, shift):
            layernorm_scale(e, steps, n, k, eps_d, st, small, scale)
            return layernorm_shift(e, steps, n, k, dis, small, scale, shift)

        ln_steps = 5 + RSQRT_STEPS

        def pairs(tiles):
            return [range(j, min(j + 2, tiles)) for j in range(0, tiles, 2)]

        def size(g):
            if isinstance(g, int) and g >= NG:
                return (1, TAIL) if g == NG else (0, 0)
            return K, P

        def node_groups(eng, group, steps=None, per_group=0):
            with eng.Fori(0, NG // RING) as i:
                if steps:
                    steps.enter(i, RING * per_group)
                for b in range(RING):
                    group(i * RING + b, i, b, K, P)
            if steps:
                steps.leave(NG // RING)
            for b in range(NG % RING + 1):
                group(NG // RING * RING + b, NG // RING, b, *size(NG // RING * RING + b))

        class LayernormNodes:

            def __init__(self, stack, name, table, eps_d, dis, ahead):
                def buf(name_, shape):
                    return stack.enter_context(nc.sbuf_tensor(name_ + name, shape, F32))

                def flag(name_):
                    return stack.enter_context(nc.semaphore(name_ + name))

                self.table, self.eps_d, self.dis, self.ahead = table, eps_d, dis, ahead
                self.rows = buf("rows", [P, RING, K, table.shape[1]])
                self.st, self.coef = buf("st", [P, RING * K, 6]), buf("coef", [P, 2, RING * K])
                self.small = buf("small", [P, RING // 2 + 1, 4, 2 * K])
                self.rows_in = [flag(f"rows_in{b}") for b in range(RING)]
                self.stats_ready, self.coef_ready = flag("stats_ready"), flag("coef_ready")

            def load(self, sp, g, i, b, tiles, n):
                sp.dma_start(self.rows[0:n, b, 0:tiles, :], node_rows(self.table, g, tiles)).then_inc(self.rows_in[b], 16)

            def stats(self, dve, g, i, b, js, n):
                dve.wait_ge(self.rows_in[b], i * 16 + 16)
                for j in js:
                    last = nc.vector.bn_stats(self.st[0:n, b * K + j, :], self.rows[0:n, b, j, 0:D])
                return last

            def norm(self, to, b, js, n):
                for j in js:
                    at = b * K + j
                    last = nc.scalar.activation(to[0:n, b, j, :], self.rows[0:n, b, j, 0:D], ACT.Relu,
                                                scale=self.coef[0:n, 0, at:at + 1], bias=self.coef[0:n, 1, at:at + 1])
                return last

            def coefficients(self, e, steps, g, b, slot, many, tiles, n, stage="both"):
                k = tiles * many
                at = slice(b * K, b * K + k)
                eps_d, dis = (a and a[0:n, bass.ds(g * K, k)] for a in (self.eps_d, self.dis))
                scale, shift = self.coef[:, 0, at], self.coef[:, 1, at]
                if stage != "shift":
                    e.wait_ge(self.stats_ready, g + many)
                    layernorm_scale(e, steps, n, k, eps_d, self.st[:, at, :], self.small[:, slot], scale)
                if stage != "scale":
                    layernorm_shift(e, steps, n, k, dis, self.small[:, slot], scale, shift
                                    ).then_inc(self.coef_ready, many)

            def pool_program(self, pool, stage, then=None, then_steps=0):
                pool_steps.eng = pool

                def pair_of_groups(g, i, b, stage):
                    if stage:
                        self.coefficients(nc.gpsimd, pool_steps, g, b, b // 2, 2, K, P, stage)
                    if then:
                        then(g, i, b, 2)

                for b in range(0, RING, 2):
                    pair_of_groups(b, 0, b, stage if b < self.ahead else "both")
                with pool.Fori(1, NG // RING) as i:
                    pool_steps.enter(i, RING // 2 * (ln_steps + then_steps), first=1)
                    for b in range(0, RING, 2):
                        pair_of_groups(i * RING + b, i, b, "both")
                pool_steps.leave(NG // RING)
                i, b = NG // RING, NG % RING - 1
                for at in range(0, b, 2):
                    pair_of_groups(i * RING + at, i, at, "both")
                self.coefficients(nc.gpsimd, pool_steps, NG - 1, b, RING // 2 - 1, 1, K, P)
                if then:
                    then(NG - 1, i, b, 1)
                self.coefficients(nc.gpsimd, pool_steps, NG, b + 1, RING // 2, 1, 1, TAIL)

        def node_group_ahead(g, i, b, m):
            to = g + m, i + (b + m) // RING, (b + m) % RING, *size(g + m)
            return to if to[3] else None

        def node_rows(table, g, tiles):
            if tiles == 1:
                return table[main:N, :].rearrange("(t p) d -> p t d", t=1)
            return rows(table)[:, bass.ds(g * K, K), :]

        nodes_1_stack = ctx.enter_context(ExitStack())
        nodes_1 = LayernormNodes(nodes_1_stack, "_n1", x, None, dis_all, AHEAD[1])
        stored = [sem(f"stored{b}") for b in range(RING)]

        with ExitStack() as ph:
            hot_q = ph.enter_context(nc.sbuf_tensor("hot_q", [P, 3, P, K], BF16))
            hot_r = ph.enter_context(nc.sbuf_tensor("hot_r", [P, 3, K, T + 1], BF16))
            iota_q = ph.enter_context(nc.sbuf_tensor("iota_q", [P, P, K], F16))
            q_short = ph.enter_context(nc.sbuf_tensor("q_short", [P, T + 1], F16))
            iota_r = ph.enter_context(nc.sbuf_tensor("iota_r", [P, T + 1], F16))
            q = ph.enter_context(nc.sbuf_tensor("q", [P, T + 1], F32))
            r = ph.enter_context(nc.sbuf_tensor("r", [P, T + 1], F32))
            t1 = ph.enter_context(nc.sbuf_tensor("t1", [P, T + 1], F32))
            i1 = ph.enter_context(nc.sbuf_tensor("i1", [P, T + 1], I32))
            rest, term = (ph.enter_context(nc.sbuf_tensor(n, [3 * Q, D], F32)) for n in ("rest", "term"))
            r_now = ph.enter_context(nc.sbuf_tensor("r_now1", [P, 3, K], F32))
            deg = ph.enter_context(nc.psum_tensor("deg", [P, 512], F32))
            edges_in, weights_in = ph.enter_context(nc.semaphore("edges_in")), sem("weights_in")
            pads_set, consts_set = ph.enter_context(nc.semaphore("pads_set")), sem("consts_set")
            rows_set = ph.enter_context(nc.semaphore("rows_set"))
            squares = ph.enter_context(nc.sbuf_tensor("squares", [P, ACT_K, T + 1], BF16))
            q_ready, r_ready = (ph.enter_context(nc.semaphore(n)) for n in ("q_ready", "r_ready"))
            squares_ready = ph.enter_context(nc.semaphore("squares_ready"))
            act_hots_ready = ph.enter_context(nc.semaphore("act_hots_ready"))
            hots_ready = ph.enter_context(nc.semaphore("hots_ready"))
            hots_used = ph.enter_context(nc.semaphore("hots_used"))
            block = ph.enter_context(nc.Block())
            PADS, CONSTS = 3, 9

            @block.sync
            def _(sp):
                sp.wait_ge(pads_set, PADS)
                for held, edges in ((src_i, src), (dst_i, dst), (ew, edge_weight)):
                    sp.dma_start(held[:, 0:T], edges[0:main].rearrange("(p t) -> p t", t=T)).then_inc(edges_in, 16)
                    sp.dma_start(held[0:TAIL, T:T + 1], edges[main:N].rearrange("(p t) -> p t", t=1)).then_inc(edges_in, 16)
                for held, w in ((w1e, we1), (w2e, we2), (w1n, wn1), (w2n, wn2)):
                    sp.dma_start(held[:, :], w[:, :]).then_inc(weights_in, 16)
                for held, b in ((b1e, be1), (b1n, bn1)):
                    sp.dma_start(held[:, :], b.rearrange("(p t) -> p t", t=1)).then_inc(weights_in, 16)
                for held, b in ((b2e, be2), (b2n, bn2)):
                    sp.dma_start(held[:, :], b.partition_broadcast(3 * Q)).then_inc(weights_in, 16)
                for b in range(RING):
                    nodes_1.load(sp, b, 0, b, K, P)
                sp.wait_ge(weights_in, 16 * 8)
                sp.wait_ge(consts_set, CONSTS)
                for b, (table, at, n) in enumerate(((z_table, N, P // 2), (z_table, N + P // 2, P // 2),
                                                    (m_table, main, TAIL // 2), (m_table, main + TAIL // 2, TAIL // 2))):
                    sp.dma_start(table[at:at + n, :], zeros[0:n, 0:table.shape[1]]).then_inc(stored[b], 16)
                for b in range(4, RING):
                    sp.dma_start(m_table[N + b:N + b + 1, :], zeros[0:1, 0:D]).then_inc(stored[b], 16)


            @block.gpsimd
            def _(pool):
                for held in (src_i, dst_i, ew):
                    nc.gpsimd.memset(held[:, T:T + 1], 0).then_inc(pads_set, 1)
                nc.gpsimd.iota(iota_q[:, :, :], [[1, P], [0, K]], base=0, channel_multiplier=0,
                               allow_small_or_imprecise_dtypes=True).then_inc(consts_set, 1)
                nc.gpsimd.iota(iota_r[:, :], [[1, T + 1]], base=0, channel_multiplier=0,
                               allow_small_or_imprecise_dtypes=True).then_inc(consts_set, 1)
                nc.gpsimd.iota(spare_row[:, :], [[0, 1]], base=N, channel_multiplier=1,
                               allow_small_or_imprecise_dtypes=True).then_inc(consts_set, 1)
                nc.gpsimd.memset(zeros[:, :], 0.0).then_inc(consts_set, 1)
                nc.gpsimd.memset(before[:, :], 1.0).then_inc(consts_set, 1)
                nc.gpsimd.memset(ident[:, :], 0.0).then_inc(consts_set, 1)
                pool.wait_ge(consts_set, 6)
                nc.gpsimd.affine_select(out=ident[:, :], in_=ident[:, :], compare_op=ALU.not_equal, fill=1.0, base=0,
                                        pattern=[[-1, P]], channel_multiplier=1).then_inc(consts_set, 1)
                for at in (0, 2 * P):
                    nc.gpsimd.affine_select(out=before[:, at:at + P], in_=before[:, at:at + P], compare_op=ALU.is_gt,
                                            fill=0.0, base=0, pattern=[[-1, P]],
                                            channel_multiplier=1).then_inc(consts_set, 1)
                pool_steps.eng = pool
                pool.wait_ge(weights_in, 16 * 8)
                for b2, terms in ((b2e, b2e_terms), (b2n, b2n_terms)):
                    pool_steps.link(nc.gpsimd.tensor_copy(rest[:, :], b2[:, :]))
                    for quadrant in range(3):
                        pool_steps.link(nc.gpsimd.tensor_copy(terms[:, 0:D], rest[:, :]))
                        for at in range(quadrant + 1, 3):
                            later = slice(at * Q, (at + 1) * Q)
                            pool_steps.link(nc.gpsimd.tensor_copy(term[later, :], terms[later, 0:D]))
                            pool_steps.link(nc.gpsimd.tensor_tensor(rest[later, :], rest[later, :], term[later, :],
                                                                    ALU.subtract))
                    pool_steps.link(nc.gpsimd.tensor_copy(terms[:, D:2 * D], terms[:, 0:D]))
                for b in range(0, AHEAD[1], 2):
                    nodes_1.coefficients(nc.gpsimd, pool_steps, b, b, b // 2, 2, K, P, "scale")

            @block.vector
            def _(dve):
                steps.eng = dve
                steps.link(nc.vector.memset(first_rows[:, :], 0.0))
                for at in range(0, 3 * Q, Q):
                    nc.vector.memset(first_rows[at:at + 1, :], 1.0).then_inc(rows_set, 1)
                dve.wait_ge(edges_in, 16 * 6)
                nc.vector.tensor_copy(src_f[:, :], src_i[:, :])
                steps.link(nc.vector.tensor_copy(dst_f[:, :], dst_i[:, :]))
                steps.link(nc.vector.tensor_scalar(i1[:, :], src_f[:, :], 1.0 / T, None, ALU.mult))
                steps.link(nc.vector.tensor_copy(q[:, :], i1[:, :]))
                steps.link(nc.vector.scalar_tensor_tensor(out=r[:, :], in0=q[:, :], scalar=-float(T), in1=src_f[:, :],
                                                          op0=ALU.mult, op1=ALU.add))
                for op, bound, sign in ((ALU.is_lt, 0.0, -1.0), (ALU.is_ge, float(T), 1.0)):
                    steps.link(nc.vector.tensor_scalar(t1[:, :], r[:, :], bound, sign, op, ALU.mult))
                    nc.vector.tensor_tensor(q[:, :], q[:, :], t1[:, :], ALU.add)
                    steps.link(nc.vector.scalar_tensor_tensor(out=r[:, :], in0=t1[:, :], scalar=-float(T),
                                                              in1=r[:, :], op0=ALU.mult, op1=ALU.add))
                steps.link(nc.vector.tensor_scalar(t1[:, :], src_f[:, :], float(main), None, ALU.is_ge))
                steps.link(nc.vector.scalar_tensor_tensor(out=d_all[:, :], in0=r[:, :], scalar=-float(P), in1=t1[:, :],
                                                          op0=ALU.add, op1=ALU.mult))
                steps.link(nc.vector.tensor_tensor(q[:, :], q[:, :], d_all[:, :], ALU.add))
                steps.link(nc.vector.scalar_tensor_tensor(out=d_all[:, :], in0=r[:, :], scalar=-float(T), in1=t1[:, :],
                                                          op0=ALU.add, op1=ALU.mult))
                steps.link(nc.vector.tensor_tensor(r[:, :], r[:, :], d_all[:, :], ALU.subtract))
                dve.wait_ge(consts_set, CONSTS)

                nc.vector.tensor_copy(q_short[:, :], q[:, :]).then_inc(q_ready, 1)
                dve.wait_ge(q_ready, 1)
                with dve.Fori(0, NG // 3) as i:
                    for b in range(3):
                        g = i * 3 + b
                        dve.wait_ge(hots_used, g + 1)
                        nc.vector.tensor_copy(r_now[:, b, :], r[:, bass.ds(g * K, K)]).then_inc(r_ready, 1)
                        nc.vector.tensor_tensor(
                            hot_q[:, b, :, :], iota_q[:, :, :],
                            q_short[:, bass.ds(g * K, K)].unsqueeze(1).to_broadcast([P, P, K]), ALU.is_equal)
                        dve.wait_ge(r_ready, g + 1)
                        for j in range(K - ACT_K):
                            last = nc.vector.tensor_scalar(hot_r[:, b, j, :], iota_r[:, :], r_now[:, b, j:j + 1], None,
                                                           ALU.is_equal)
                        last.then_inc(hots_ready, 1)
                dve.wait_ge(hots_used, NG + 1)
                nc.vector.tensor_scalar(hot_q[0:TAIL, 0, :, 0], iota_q[0:TAIL, :, 0], q[0:TAIL, T:T + 1], None,
                                        ALU.is_equal)
                nc.vector.tensor_scalar(hot_r[0:TAIL, 0, 0, :], iota_r[0:TAIL, :], r[0:TAIL, T:T + 1], None,
                                        ALU.is_equal).then_inc(hots_ready, 1)

                for b in range(AHEAD[1]):
                    nodes_1.stats(dve, b, 0, b, range(K), P).then_inc(nodes_1.stats_ready, 1)
                steps.link(nc.vector.tensor_tensor(t1[:, :], src_f[:, :], dst_f[:, :], ALU.not_equal))
                steps.link(nc.vector.tensor_tensor(ew[:, :], ew[:, :], t1[:, :], ALU.mult))
                dve.wait_ge(hots_used, NG + 4)
                nc.vector.tensor_scalar(t1[:, :], deg[:, 0:T + 1], 1.0, None, ALU.min)
                steps.link(nc.vector.tensor_scalar(d_all[:, :], deg[:, 0:T + 1], 1.0, None, ALU.max))
                rsqrt(nc.vector, steps, r_all[:, :], d_all[:, :], q[:, :])
                nc.vector.tensor_scalar(eps_d_all[:, :], d_all[:, :], EPS, None, ALU.mult)
                nc.vector.tensor_tensor(s_all[:, :], d_all[:, :], r_all[:, :], ALU.mult)
                steps.link(nc.vector.tensor_tensor(dis_all[:, :], t1[:, :], r_all[:, :], ALU.mult))

            @block.tensor
            def _(pe):
                pe.wait_ge(consts_set, CONSTS)
                pe.wait_ge(rows_set, 3)
                nc.tensor.matmul(deg[:, 0:T + 1], first_rows[:, :],
                                 zeros[0:3 * Q, 0:T + 1].bitcast(BF16)[:, 0:T + 1],
                                 start=True, stop=False, skip_group_check=True)

                pe.sem_inc(hots_used, 3)

                def count(g, b, tiles, n, last_of_all=False):
                    pe.wait_ge(hots_ready, g + 1)
                    for j in range(tiles):
                        if j == K - ACT_K:
                            pe.wait_ge(act_hots_ready, g + 1)
                        last = nc.tensor.matmul(deg[:, 0:T + 1], hot_q[0:n, b, :, j], hot_r[0:n, b, j, :],
                                                start=False, stop=last_of_all, skip_group_check=True)
                    last.then_inc(hots_used, 1)

                with pe.Fori(0, NG // 3) as i:
                    for b in range(3):
                        count(i * 3 + b, b, K, P)
                count(NG, 0, 1, TAIL, last_of_all=True)

            @block.scalar
            def _(act):
                act.wait_ge(consts_set, CONSTS)
                with act.Fori(0, NG // 3) as i:
                    for b in range(3):
                        g = i * 3 + b
                        act.wait_ge(r_ready, g + 1)
                        for m in range(ACT_K):
                            at = K - ACT_K + m
                            last = nc.scalar.activation(squares[:, m, :], iota_r[:, :], ACT.Square,
                                                        scale=-1.0, bias=r_now[:, b, at:at + 1])
                        last.then_inc(squares_ready, 1)
                        act.wait_ge(squares_ready, g + 1)
                        nc.scalar.activation(hot_r[:, b, K - ACT_K:K, :], squares[:, :, :], ACT.Relu,
                                             scale=-1.0, bias=1.0).then_inc(act_hots_ready, 1)
                        act.wait_ge(act_hots_ready, g + 1)

        with ExitStack() as ph:
            def buf(name, shape, dt=F32):
                return ph.enter_context(nc.sbuf_tensor(name, shape, dt))

            def flag(name):
                return ph.enter_context(nc.semaphore(name))

            gt, zt = buf("gt", [P, RING, K, D]), buf("zt", [P, RING, K, ZW])
            s_now = buf("s_now", [P, RING, K])
            xt, g_ready = nodes_1.rows, flag("g_ready")
            z_ready = flag("z_ready")
            fill_set = flag("fill_set2")
            block = ph.enter_context(nc.Block())

            @block.sync
            def _(sp):
                def group(g, i, b, tiles, n):
                    sp.wait_ge(z_ready, g + 1)
                    if to := node_group_ahead(g, i, b, RING):
                        nodes_1.load(sp, *to)
                    sp.dma_start(node_rows(g_table, g, tiles), gt[0:n, b, 0:tiles, :]).then_inc(stored[b], 16)
                    sp.dma_start(node_rows(z_table[0:N, :], g, tiles), zt[0:n, b, 0:tiles, :]).then_inc(stored[b], 16)

                with sp.Fori(0, NG // RING - 1) as i:
                    for b in range(RING):
                        group(i * RING + b, i, b, K, P)
                for g in range((NG // RING - 1) * RING, NG + 1):
                    group(g, g // RING, g % RING, *size(g))
                for b in range(RING):
                    sp.wait_ge(stored[b], 16 + 32 * len(range(b, NG + 1, RING)))

            @block.vector
            def _(dve):
                steps.eng = dve
                for b in range(RING):
                    nc.vector.memset(zt[:, b, :, D + 1:ZW], 0.0).then_inc(fill_set, 1)

                def group(g, i, b, tiles, n):
                    if to := node_group_ahead(g, i, b, AHEAD[1]):
                        nodes_1.stats(dve, *to[:3], range(to[3]), to[4]).then_inc(nodes_1.stats_ready, 1)
                    dve.wait_ge(stored[b], i * 32 + 16)
                    nc.vector.tensor_copy(zt[0:n, b, 0:tiles, D], d_all[0:n, bass.ds(g * K, tiles)])
                    steps.link(nc.vector.tensor_copy(s_now[0:n, b, 0:tiles], s_all[0:n, bass.ds(g * K, tiles)]))
                    dve.wait_ge(g_ready, g + 1)
                    for j in range(tiles):
                        last = nc.vector.scalar_tensor_tensor(
                            out=zt[0:n, b, j, 0:D], in0=xt[0:n, b, j, :], scalar=s_now[0:n, b, j:j + 1],
                            in1=gt[0:n, b, j, :], op0=ALU.mult, op1=ALU.add)
                    last.then_inc(z_ready, 1)

                node_groups(dve, group, steps, 1)

            @block.gpsimd
            def _(pool):
                nodes_1.pool_program(pool, "shift")

            @block.scalar
            def _(act):
                def group(g, i, b, tiles, n):
                    act.wait_ge(nodes_1.coef_ready, g + 1)
                    act.wait_ge(stored[b], i * 32 + 16)
                    nodes_1.norm(gt, b, range(tiles), n).then_inc(g_ready, 1)

                node_groups(act, group)

        def edge_layer(layer):
            mlp = layer == 2
            table, width, gather_i = (z_table, ZW, src_i) if mlp else (g_table, D, dst_i)
            key_f, keys_by_tile = (dst_f, dst_by_tile) if mlp else (src_f, src_by_tile)
            sums_table, sum_width = (m_table, D) if mlp else (z_table, ZW)
            with ExitStack() as ph:
                def buf(name, shape, dt=F32):
                    return ph.enter_context(nc.sbuf_tensor(f"{name}_{layer}", shape, dt))

                def bank(name):
                    return ph.enter_context(nc.psum_tensor(f"{name}_{layer}", [P, 2 * P], F32))

                def flag(name):
                    return ph.enter_context(nc.semaphore(f"{name}_{layer}"))

                got = buf("got", [P, 2, K, width])
                sums = buf("sums", [P, 2, K, sum_width])
                spread = buf("spread", [P, 2, K * P], I32)
                same = buf("same", [P, 2, PAIRS, 3 * P])
                dup = buf("dup", [P, K])
                junk = buf("junk", [P, 2, 3 * P], BF16)
                gather_at, sums_at = buf("gather_at", [P, 2, K], I32), buf("sums_at", [P, 2, K], I32)
                key, weight = buf("key", [P, 2, K]), buf("weight", [P, 2, K])
                detour = buf("detour", [P, K])
                pair_sums = [bank(f"pair_sums{b}") for b in range(2)]
                indices_staged = flag("indices_staged")
                spread_in = [flag(f"spread_in{b}") for b in range(2)]
                look = 2 if mlp else 1
                gathered = [[flag(f"gathered{b}_{k}") for k in range(1 if mlp else PAIRS)] for b in range(2)]
                compared = flag("compared")
                rows_picked = flag("rows_picked")
                summed = flag("summed")
                sums_ready = flag("sums_ready")
                sums_added = flag("sums_added")
                added = flag("added")
                waited = flag("waited")
                if mlp:
                    ea = buf("ea", [DE, 2, K * P])
                    hidden = buf("hidden", [P, 2, 2 * P])
                    normed = buf("normed", [P, 2, K, D])
                    message = buf("message", [P, 2, 2, D])
                    st, small, coef = buf("st", [P, K, 6]), buf("small", [P, 4, K]), buf("coef", [P, 2, 2, K])
                    eps_d = buf("eps_d", [P, K])
                    hidden_p = [bank(f"hidden_p{b}") for b in range(2)]
                    filter_p = [bank(f"filter_p{b}") for b in range(2)]
                    ea_in = [flag(f"ea_in{b}") for b in range(2)]
                    hid_summed = flag("hid_summed")
                    hid_ready = flag("hid_ready")
                    filter_ready, message_ready = flag("filter_ready"), flag("message_ready")
                    coef_ready, normed_ready = flag("coef_ready"), flag("normed_ready")
                else:
                    cleared, fill_set = flag("cleared"), flag("fill_set")
                block = ph.enter_context(nc.Block())

                def pairs(tiles):
                    return [range(j, min(j + 2, tiles)) for j in range(0, tiles, 2)]

                def groups(eng, group, per_turn=None):
                    with eng.Fori(0, NG // 2 - 1) as i:
                        if per_turn is not None:
                            steps.enter(i, per_turn)
                        for b in range(2):
                            group(i * 2 + b, i, b, K, P)
                    if per_turn is not None:
                        steps.leave(NG // 2 - 1)
                    for g in range(NG - 3, NG + 1):
                        group(g, g // 2, g % 2, *size(g))

                def size(g):
                    if isinstance(g, int) and g >= NG:
                        return (1, TAIL) if g == NG else (0, 0)
                    return K, P

                def pair_ahead(g, i, b, k, m):
                    g, i, b, k = (g + 1, i + b, 1 - b, k + m - PAIRS) if k + m >= PAIRS else (g, i, b, k + m)
                    tiles, n = size(g)
                    return (g * PAIRS + k, g, i, b, k, pairs(tiles)[k], n) if k < len(pairs(tiles)) else None

                @block.sync
                def _(sp):
                    def group(g, i, b, tiles, n):
                        def edges(k, pair):
                            return (slice(2 * k * P, 2 * k * P + len(pair) * n),
                                    bass.ds(g * (K * P) + 2 * k * P, len(pair) * n))

                        for k, pair in enumerate(pairs(tiles)):
                            held, at = edges(k, pair)
                            sp.wait_ge(added, g * PAIRS + (k + PACE[layer]))
                            sp.sem_inc(waited, 1)
                            sp.wait_ge(compared, g * PAIRS + (k + 1))
                            sp.sem_inc(waited, 1)
                            sp.dma_start(spread[:, b, held],
                                         keys_by_tile[at].partition_broadcast(P)).then_inc(spread_in[b], 16)
                            if not mlp and tiles == K:
                                sp.dma_start(rows(m_table)[:, bass.ds(g * K + 2 * k, 2), :],
                                             zeros[:, 0:2 * D].rearrange("p (k d) -> p k d", d=D)).then_inc(cleared, 16)
                        if mlp:
                            for k, pair in enumerate(pairs(tiles)):
                                held, at = edges(k, pair)
                                sp.wait_ge(hid_summed, g * PAIRS + (k + 1))
                                sp.sem_inc(waited, 1)
                                sp.dma_start(ea[:, b, held], attr_t[:, at]).then_inc(ea_in[b], 16)

                    groups(sp, group)
                    if mlp:
                        for b in range(RING):
                            nodes_2.load(sp, b, 0, b, K, P)
                    else:
                        sp.wait_ge(cleared, 16 * NG * PAIRS)

                @block.gpsimd
                def _(pool):
                    pool.sem_inc(added, 3 * PAIRS - 1)
                    at = N + (P // 2 if mlp else 0)
                    pool.dma_start(m_table[at:at + P // 2, :], zeros[0:P // 2, 0:D]).then_inc(sums_added, 16)

                    def gather(b, j, n):
                        got_in = gathered[b][0 if mlp else j // 2]
                        pool.indirect_dma_start(got[0:n, b, j, :], None, table[:, :],
                                                bass.IndirectOffsetOnAxis(gather_at[0:n, b, j:j + 1], axis=0)
                                                ).then_inc(got_in, 16)

                    def group(g, i, b, tiles, n):
                        ahead, ahead_n = size(g + look)
                        to = b if mlp else 1 - b
                        for k, pair in enumerate(pairs(tiles)):
                            if k == 0 and ahead:
                                pool.wait_ge(indices_staged, g + (look + 1))
                                if mlp:
                                    pool.wait_ge(normed_ready, g + 1)
                                else:
                                    pool.wait_ge(summed, g * PAIRS + (PAIRS + 1))
                                pool.sem_inc(waited, 1)
                            for j in pair:
                                if j < ahead:
                                    gather(to, j, ahead_n)
                            pool.wait_ge(sums_added, (g * PAIRS + k) * 32 + 16)
                            pool.sem_inc(added, 1)
                            if k == 0:
                                pool.wait_ge(rows_picked, g + 1)
                            pool.wait_ge(sums_ready, g * PAIRS + (k + 3))
                            pool.sem_inc(waited, 1)
                            for j in pair:
                                pool.indirect_dma_start(
                                    sums_table[:, :], bass.IndirectOffsetOnAxis(sums_at[0:n, b, j:j + 1], axis=0),
                                    sums[0:n, b, j, :], None, compute_op=ALU.add).then_inc(sums_added, 16)

                    for g in range(look):
                        pool.wait_ge(indices_staged, g + 1)
                        for j in range(K):
                            gather(g, j, P)
                    groups(pool, group)
                    pool.wait_ge(sums_added, 16 * (T + 2))

                @block.vector
                def _(dve):
                    steps.eng = dve
                    dve.sem_inc(compared, PAIRS + 1)
                    if mlp:
                        dve.sem_inc(message_ready, 2)

                    def stage_indices(g, b, tiles, n):
                        nc.vector.tensor_copy(gather_at[0:n, b, 0:tiles],
                                              gather_i[0:n, bass.ds(g * K, tiles)]).then_inc(indices_staged, 1)

                    def stage_keys(g, i, b, tiles, n):
                        cols = bass.ds(g * K, tiles)
                        if not mlp:
                            nc.vector.tensor_copy(weight[0:n, b, 0:tiles], ew[0:n, cols])
                        steps.link(nc.vector.tensor_copy(key[0:n, b, 0:tiles], key_f[0:n, cols]))
                        dve.wait_ge(spread_in[b], i * 16 * PAIRS + 16 * len(pairs(tiles)))
                        dve.wait_ge(summed, g * PAIRS + 1)

                    def compare(g, b, k, tiles, n):
                        dve.wait_ge(compared, g * PAIRS + (k + PAIRS))
                        for m, j in enumerate(pairs(tiles)[k]):
                            others = n if tiles == 1 else (m + 1) * P
                            at = m * P
                            mine, theirs = key[0:n, b, j:j + 1], spread[0:n, b, 2 * k * P:2 * k * P + others]
                            if mlp:
                                nc.vector.tensor_scalar(same[0:n, b, k, at:at + others], theirs, mine, None,
                                                        ALU.is_equal)
                            else:
                                nc.vector.tensor_scalar(same[0:n, b, k, at:at + others], theirs, mine,
                                                        weight[0:n, b, j:j + 1], ALU.is_equal, ALU.mult)
                            last = nc.vector.scalar_tensor_tensor(
                                out=junk[0:n, (b + k) % 2, at:at + others], in0=theirs, scalar=mine,
                                in1=before[0:n, at:at + others], op0=ALU.is_equal, op1=ALU.mult,
                                accum_out=dup[0:n, j:j + 1])
                        last.then_inc(compared, 1)

                    def pick_rows(g, b, tiles, n):
                        dve.wait_ge(compared, g * PAIRS + (len(pairs(tiles)) + PAIRS + 1))
                        mine, many, way = key[0:n, b, 0:tiles], dup[0:n, 0:tiles], detour[0:n, 0:tiles]
                        steps.link(nc.vector.tensor_scalar(way, mine, -1.0, spare_row[0:n, :], ALU.mult, ALU.add))
                        steps.link(nc.vector.scalar_tensor_tensor(out=way, in0=many, scalar=1.0, in1=way,
                                                                  op0=ALU.min, op1=ALU.mult))
                        dve.wait_ge(added, g * PAIRS + 2 * PAIRS)
                        nc.vector.tensor_tensor(sums_at[0:n, b, 0:tiles], mine, way, ALU.add).then_inc(rows_picked, 1)

                    def norm(g, i, b, tiles, n):
                        dve.wait_ge(gathered[b][0], i * 16 * K + 16 * tiles)
                        nc.vector.tensor_scalar(eps_d[0:n, 0:tiles], got[0:n, b, 0:tiles, D], EPS, None, ALU.mult)
                        for j in range(tiles):
                            last = nc.vector.bn_stats(st[0:n, j, :], got[0:n, b, j, 0:D])
                        steps.link(last)
                        layernorm_coefficients(nc.vector, steps, n, tiles, eps_d[0:n, 0:tiles], None, st, small,
                                               coef[:, b, 0, :], coef[:, b, 1, :]).then_inc(coef_ready, 1)

                    def send(g, b, k, pair, n):
                        p = g * PAIRS + k
                        if k == 0:
                            dve.wait_ge(normed_ready, g + 1)
                        dve.wait_ge(filter_ready, p + 3)
                        dve.wait_ge(summed, p + PAIRS)
                        nc.vector.tensor_tensor(
                            message[0:n, (b + k) % 2, 0:len(pair), :], normed[0:n, b, pair[0]:pair[-1] + 1, :],
                            filter_p[(b + k) % 2][0:n, 0:len(pair) * D].rearrange("p (j d) -> p j d", d=D),
                            ALU.mult).then_inc(message_ready, 1)

                    def group(g, i, b, tiles, n):
                        nxt, nxt_n = size(g + 1)
                        if size(g + 2)[0]:
                            if not mlp:
                                for got_in in gathered[b]:
                                    dve.wait_ge(got_in, i * 32 + 32)
                            stage_indices(g + 2, b, *size(g + 2))
                        if nxt:
                            dve.wait_ge(rows_picked, g + 1)
                            stage_keys(g + 1, i + b, 1 - b, nxt, nxt_n)
                        for k in range(PAIRS):
                            if mlp and k < len(pairs(tiles)):
                                send(g, b, k, pairs(tiles)[k], n)
                            if k < len(pairs(nxt)):
                                compare(g + 1, 1 - b, k, nxt, nxt_n)
                            if mlp and nxt and k == 2:
                                norm(g + 1, i + b, 1 - b, nxt, nxt_n)
                        if nxt:
                            pick_rows(g + 1, 1 - b, nxt, nxt_n)

                    for g in range(2):
                        stage_indices(g, g, K, P)
                    stage_keys(0, 0, 0, K, P)
                    for k in range(PAIRS):
                        compare(0, 0, k, K, P)
                    pick_rows(0, 0, K, P)
                    if mlp:
                        norm(0, 0, 0, K, P)
                    groups(dve, group, 2 * (3 + (1 + ln_steps if mlp else 0)))
                    if mlp:
                        for b in range(AHEAD[2]):
                            nodes_2.stats(dve, b, 0, b, range(K), P).then_inc(nodes_2.stats_ready, 1)
                        for b in range(0, AHEAD[2], 2):
                            nodes_2.coefficients(nc.vector, steps, b, b, b // 2, 2, K, P)

                @block.scalar
                def _(act):
                    act.sem_inc(sums_ready, 2)
                    if mlp:
                        act.sem_inc(hid_ready, 2)
                    else:
                        for b in range(2):
                            nc.scalar.activation(sums[:, b, :, D:ZW], zeros[:, 0:K * (ZW - D)].rearrange(
                                "p (k d) -> p k d", k=K), ACT.Copy).then_inc(fill_set, 1)
                        act.wait_ge(fill_set, 2)

                    def norm(g, b, tiles, n):
                        act.wait_ge(coef_ready, g + 1)
                        for j in range(tiles):
                            last = nc.scalar.activation(
                                normed[0:n, b, j, :], got[0:n, b, j, 0:D], ACT.Relu,
                                scale=coef[0:n, b, 0, j:j + 1], bias=coef[0:n, b, 1, j:j + 1])
                        last.then_inc(normed_ready, 1)

                    def hide(p, g, i, b, k, pair, n):
                        act.wait_ge(hid_summed, p + (PAIRS + 2))
                        act.wait_ge(filter_ready, p + 1)
                        nc.scalar.activation(hidden[:, (b + k) % 2, 0:len(pair) * n],
                                             hidden_p[(b + k) % 2][:, 0:len(pair) * n], ACT.Silu,
                                             bias=b1e[:, 0:1]).then_inc(hid_ready, 1)

                    def group(g, i, b, tiles, n):
                        for k, pair in enumerate(pairs(tiles)):
                            p = g * PAIRS + k
                            if mlp and (to := pair_ahead(g, i, b, k, 2)):
                                hide(*to)
                            act.wait_ge(summed, p + (PAIRS + 2))
                            act.wait_ge(added, p + (PAIRS + 1))
                            nc.scalar.activation(
                                sums[0:n, b, pair[0]:pair[-1] + 1, 0:D],
                                pair_sums[(b + k) % 2][0:n, 0:len(pair) * D].rearrange("p (j d) -> p j d", d=D),
                                ACT.Copy).then_inc(sums_ready, 1)
                            if mlp and k == 3 and size(g + 1)[0]:
                                norm(g + 1, 1 - b, *size(g + 1))

                    if mlp:
                        hide(*pair_ahead(0, 0, 0, 0, 0))
                        hide(*pair_ahead(0, 0, 0, 0, 1))
                        norm(0, 0, K, P)
                    groups(act, group)
                    if mlp:
                        act.wait_ge(nodes_2.coef_ready, 1)
                        nodes_2.norm(on, 0, range(ACT_TILES), P).then_inc(h_ready, 1)

                @block.tensor
                def _(pe):
                    pe.sem_inc(summed, PAIRS + 1)
                    if mlp:
                        pe.sem_inc(hid_summed, PAIRS + 1)
                        pe.sem_inc(filter_ready, 2)

                    def hide(p, g, i, b, k, pair, n):
                        if k == 0:
                            pe.wait_ge(ea_in[b], i * 16 * PAIRS + 16 * len(pairs(size(g)[0])))
                        pe.wait_ge(hid_ready, p + 1)
                        cols = len(pair) * n
                        nc.tensor.matmul(hidden_p[(b + k) % 2][:, 0:cols], w1e[:, :],
                                         ea[:, b, 2 * k * P:2 * k * P + cols],
                                         start=True, stop=True).then_inc(hid_summed, 1)

                    def make_filter(p, g, i, b, k, pair, n):
                        bank_ = filter_p[(b + k) % 2]
                        pe.wait_ge(message_ready, p + 1)
                        nc.tensor.matmul(bank_[0:n, 0:len(pair) * D], first_rows[:, 0:n], b2e_terms[:, 0:len(pair) * D],
                                         start=True, stop=False, skip_group_check=True)
                        pe.wait_ge(hid_ready, p + 3)
                        for m in range(len(pair)):
                            last = nc.tensor.matmul(bank_[0:n, m * D:(m + 1) * D],
                                                    hidden[:, (b + k) % 2, m * n:(m + 1) * n], w2e[:, :],
                                                    start=False, stop=(m == len(pair) - 1), skip_group_check=True)
                        last.then_inc(filter_ready, 1)

                    def group(g, i, b, tiles, n):
                        for k, pair in enumerate(pairs(tiles)):
                            p = g * PAIRS + k
                            if mlp:
                                if to := pair_ahead(g, i, b, k, 2):
                                    hide(*to)
                                if to := pair_ahead(g, i, b, k, 1):
                                    make_filter(*to)
                                pe.wait_ge(message_ready, p + 3)
                                data = [message[0:n, (b + k) % 2, m, :] for m in range(len(pair))]
                            else:
                                pe.wait_ge(gathered[b][k], i * 32 + 16 * len(pair))
                                data = [got[0:n, b, j, :] for j in pair]
                            pe.wait_ge(compared, p + (PAIRS + 2))
                            pe.wait_ge(sums_ready, p + 1)
                            bank_, same_ = pair_sums[(b + k) % 2], same[0:n, b, k, :]
                            last = nc.tensor.matmul(bank_[0:n, 0:D], same_[:, 0:n], data[0],
                                                    start=True, stop=(len(pair) == 1))
                            if len(pair) == 2:
                                nc.tensor.matmul(bank_[:, 0:D], same_[:, P:2 * P], data[1], start=False, stop=True)
                                last = nc.tensor.matmul(bank_[:, D:2 * D], same_[:, 2 * P:3 * P], data[1],
                                                        start=True, stop=True)
                            last.then_inc(summed, 1)

                    if mlp:
                        hide(*pair_ahead(0, 0, 0, 0, 0))
                        hide(*pair_ahead(0, 0, 0, 0, 1))
                        make_filter(*pair_ahead(0, 0, 0, 0, 0))
                    groups(pe, group)

        nodes_1_stack.close()
        edge_layer(1)
        nodes_2 = LayernormNodes(ctx, "_n2", z_table[0:N, :], eps_d_all, None, AHEAD[2])
        on = sb("on", [P, RING, K, D])
        h_ready, pool_h_ready = sem("h_ready"), sem("pool_h_ready")
        edge_layer(2)

        with ExitStack() as ph:
            def buf(name, shape, dt=F32):
                return ph.enter_context(nc.sbuf_tensor(name, shape, dt))

            def flag(name):
                return ph.enter_context(nc.semaphore(name))

            def banks(name):
                return [ph.enter_context(nc.psum_tensor(f"{name}{b}", [P, 2 * P], F32)) for b in range(2)]

            mn, r_now = buf("mn", [P, RING, K, D]), buf("r_now", [P, RING, K])
            x1 = buf("x1", [P, RING // 2, 2, K - ACT_TILES, D])
            zn = nodes_2.rows
            mt, hidden = buf("mt", [P, 2, 2 * P]), buf("hidden5", [P, 2, 2 * P])
            mt_p, hidden_p, out_p = banks("mt_p"), banks("hidden5_p"), banks("out_p")
            sums_in = [flag(f"sums_in{b}") for b in range(RING)]
            rows_out = [flag(f"rows_out{b}") for b in range(RING)]
            out_ready, r_staged = flag("out_ready"), flag("r_staged")
            turned, mt_ready = flag("turned"), flag("mt_ready")
            hid_summed, hid_ready = flag("hid5_summed"), flag("hid5_ready")
            branch_summed, branch_added = flag("branch_summed"), flag("branch_added")
            block = ph.enter_context(nc.Block())

            def pair_ahead(g, i, b, k, m):
                if k + m >= PAIRS:
                    g, i, b, k = g + 1, i + (b + 1) // RING, (b + 1) % RING, k + m - PAIRS
                else:
                    k = k + m
                tiles, n = size(g)
                return (g * PAIRS + k, i, b, k, pairs(tiles)[k], n) if k < len(pairs(tiles)) else None

            @block.sync
            def _(sp):
                def load(g, i, b, tiles, n):
                    sp.dma_start(mn[0:n, b, 0:tiles, :], node_rows(m_table[0:N, :], g, tiles)).then_inc(sums_in[b], 16)

                for b in range(RING):
                    load(b, 0, b, K, P)
                    if b == 0:
                        for spare in range(RING):
                            sp.dma_start(z_table[N + spare:N + spare + 1, :], zeros[0:1, 0:ZW]
                                         ).then_inc(rows_out[spare], 16)

                def group(g, i, b, tiles, n):
                    sp.wait_ge(out_ready, g + 1)
                    if to := node_group_ahead(g, i, b, RING):
                        load(*to)
                        nodes_2.load(sp, *to)
                    sp.dma_start(node_rows(out, g, tiles), on[0:n, b, 0:tiles, :]).then_inc(rows_out[b], 16)

                with sp.Fori(0, NG // RING - 1) as i:
                    for b in range(RING):
                        group(i * RING + b, i, b, K, P)
                for g in range((NG // RING - 1) * RING, NG + 1):
                    group(g, g // RING, g % RING, *size(g))
                for b in range(RING):
                    sp.wait_ge(rows_out[b], 16 + 16 * len(range(b, NG + 1, RING)))

            @block.gpsimd
            def _(pool):
                def norm(g, i, b, many):
                    pool.wait_ge(nodes_2.coef_ready, g + many)
                    for m in range(many):
                        pool.wait_ge(rows_out[b + m], i * 16 + 16)
                    pool.sem_inc(pool_waited, 1)
                    here, x1_ = on[:, b:b + many, ACT_TILES:K, :], x1[:, b // 2, 0:many, :, :]
                    for m in range(many):
                        for j in range(ACT_TILES, K):
                            at = (b + m) * K + j
                            nc.gpsimd.tensor_scalar(on[:, b + m, j, :], zn[:, b + m, j, 0:D],
                                                    nodes_2.coef[:, 0, at:at + 1], nodes_2.coef[:, 1, at:at + 1],
                                                    ALU.mult, ALU.add)
                    for m in range(many):
                        columns = bass.ds((g + m) * K + ACT_TILES, K - ACT_TILES)
                        last = nc.gpsimd.tensor_tensor(
                            x1_[:, m, :, :], zn[:, b + m, ACT_TILES:K, 0:D],
                            r_all[:, columns].unsqueeze(2).to_broadcast([P, K - ACT_TILES, D]), ALU.mult)
                    pool_steps.link(last, scalar=True)
                    pool_steps.link(nc.gpsimd.tensor_scalar(here, here, 0.0, None, ALU.max))
                    nc.gpsimd.tensor_tensor(here, here, x1_, ALU.add).then_inc(pool_h_ready, many)

                nodes_2.pool_program(pool, None, norm, 2)

            @block.vector
            def _(dve):
                steps.eng = dve
                dve.sem_inc(branch_added, 2)

                def stage_r(g, i, b, tiles, n):
                    nc.vector.tensor_copy(r_now[0:n, b, 0:tiles],
                                          r_all[0:n, bass.ds(g * K, tiles)]).then_inc(r_staged, 1)

                def group(g, i, b, tiles, n):
                    def add_x1(k):
                        dve.wait_ge(branch_added, g * PAIRS + (k + 3))
                        for j in pairs(tiles)[k]:
                            last = nc.vector.scalar_tensor_tensor(
                                out=on[0:n, b, j, :], in0=zn[0:n, b, j, 0:D], scalar=r_now[0:n, b, j:j + 1],
                                in1=on[0:n, b, j, :], op0=ALU.mult, op1=ALU.add)
                        return last

                    if to := node_group_ahead(g, i, b, 1):
                        stage_r(*to)
                    dve.wait_ge(r_staged, g + 1)
                    dve.wait_ge(h_ready, g + 1)
                    ahead = node_group_ahead(g, i, b, AHEAD[2])
                    for k, js in enumerate(pairs(tiles)):
                        here = on[0:n, b, js[0]:js[-1] + 1, :]
                        if js[0] == ACT_TILES:
                            dve.wait_ge(pool_h_ready, g + 1)
                        dve.wait_ge(branch_summed, g * PAIRS + (k + 3))
                        nc.vector.tensor_tensor(here, out_p[(b + k) % 2][0:n, 0:len(js) * D].rearrange(
                            "p (j d) -> p j d", d=D), here, ALU.add).then_inc(branch_added, 1)
                        if k:
                            last = add_x1(k - 1)
                            if js[0] == ACT_TILES:
                                last.then_inc(out_ready, 1)
                        if ahead and k < len(pairs(ahead[3])):
                            last = nodes_2.stats(dve, *ahead[:3], pairs(ahead[3])[k], ahead[4])
                            if k == len(pairs(ahead[3])) - 1:
                                last.then_inc(nodes_2.stats_ready, 1)
                    if tiles == 1:
                        add_x1(0).then_inc(out_ready, 1)

                stage_r(0, 0, 0, K, P)
                node_groups(dve, group)

            @block.scalar
            def _(act):
                act.sem_inc(hid_ready, 2)

                def turn(p, i, b, k, js, n):
                    act.wait_ge(turned, p + 1)
                    act.wait_ge(hid_summed, p + 1)
                    nc.scalar.activation(mt[:, (b + k) % 2, 0:len(js) * n], mt_p[(b + k) % 2][:, 0:len(js) * n],
                                         ACT.Copy).then_inc(mt_ready, 1)

                def hide(p, i, b, k, js, n):
                    act.wait_ge(hid_summed, p + 3)
                    act.wait_ge(branch_summed, p + 1)
                    nc.scalar.activation(hidden[:, (b + k) % 2, 0:len(js) * n], hidden_p[(b + k) % 2][:, 0:len(js) * n],
                                         ACT.Silu, bias=b1n[:, 0:1]).then_inc(hid_ready, 1)

                def norm_turns(tiles):
                    mine = range(min(tiles, ACT_TILES))
                    cuts = [len(mine) * k // PAIRS for k in range(PAIRS + 1)] if tiles == K else [0] + [1] * PAIRS
                    return [mine[cuts[k]:cuts[k + 1]] for k in range(PAIRS)]

                def group(g, i, b, tiles, n):
                    nxt = node_group_ahead(g, i, b, 1)
                    for k in range(len(pairs(tiles))):
                        if to := pair_ahead(g, i, b, k, 2):
                            turn(*to)
                        if to := pair_ahead(g, i, b, k, 1):
                            hide(*to)
                        if nxt and (js := norm_turns(nxt[3])[k]):
                            if k == 0:
                                act.wait_ge(nodes_2.coef_ready, g + 2)
                                act.wait_ge(rows_out[nxt[2]], nxt[1] * 16 + 16)
                            last = nodes_2.norm(on, nxt[2], js, nxt[4])
                            if js[-1] == min(nxt[3], ACT_TILES) - 1:
                                last.then_inc(h_ready, 1)

                turn(*pair_ahead(0, 0, 0, 0, 0))
                turn(*pair_ahead(0, 0, 0, 0, 1))
                hide(*pair_ahead(0, 0, 0, 0, 0))
                node_groups(act, group)

            @block.tensor
            def _(pe):
                pe.sem_inc(hid_summed, 2)
                pe.sem_inc(branch_summed, 2)

                def turn(p, i, b, k, js, n):
                    if k == 0:
                        pe.wait_ge(sums_in[b], i * 16 + 16)
                    for m, j in enumerate(js):
                        last = nc.tensor.transpose(mt_p[(b + k) % 2][:, m * n:(m + 1) * n], mn[0:n, b, j, :],
                                                   ident[0:n, 0:n])
                    last.then_inc(turned, 1)

                def hide(p, i, b, k, js, n):
                    pe.wait_ge(mt_ready, p + 1)
                    pe.wait_ge(hid_ready, p + 1)
                    nc.tensor.matmul(hidden_p[(b + k) % 2][:, 0:len(js) * n], w1n[:, :],
                                     mt[:, (b + k) % 2, 0:len(js) * n],
                                     start=True, stop=True).then_inc(hid_summed, 1)

                def group(g, i, b, tiles, n):
                    for k, js in enumerate(pairs(tiles)):
                        p, bank_ = g * PAIRS + k, out_p[(b + k) % 2]
                        if to := pair_ahead(g, i, b, k, 2):
                            turn(*to)
                        if to := pair_ahead(g, i, b, k, 1):
                            hide(*to)
                        pe.wait_ge(branch_added, p + 1)
                        nc.tensor.matmul(bank_[0:n, 0:len(js) * D], first_rows[:, 0:n], b2n_terms[:, 0:len(js) * D],
                                         start=True, stop=False, skip_group_check=True)
                        pe.wait_ge(hid_ready, p + 3)
                        for m in range(len(js)):
                            last = nc.tensor.matmul(bank_[0:n, m * D:(m + 1) * D],
                                                    hidden[:, (b + k) % 2, m * n:(m + 1) * n], w2n[:, :],
                                                    start=False, stop=(m == len(js) - 1), skip_group_check=True)
                        last.then_inc(branch_summed, 1)

                turn(*pair_ahead(0, 0, 0, 0, 0))
                turn(*pair_ahead(0, 0, 0, 0, 1))
                hide(*pair_ahead(0, 0, 0, 0, 0))
                node_groups(pe, group)


INPUTS = ["x", "src", "dst", "src_by_tile", "dst_by_tile", "attr_t", "edge_weight", "L1_gnn_We1", "L1_gnn_be1",
          "L1_gnn_We2", "L1_gnn_be2", "L1_gnn_Wn1", "L1_gnn_bn1", "L1_gnn_Wn2", "L1_gnn_bn2"]


def kernel(**inputs):
    import numpy as np
    import concourse.bacc as bacc
    from concourse.bass_utils import run_bass_kernel_spmd

    def by_tile(a):
        a = np.asarray(a)
        full = a[:P * T].reshape(P, T, *a.shape[1:]).swapaxes(0, 1)
        return np.concatenate([full.reshape(P * T, *a.shape[1:]), a[P * T:]])

    inputs["src_by_tile"] = by_tile(inputs["src"])
    inputs["dst_by_tile"] = by_tile(inputs["dst"])
    inputs["attr_t"] = by_tile(inputs["edge_attr_50"]).T
    nc = bacc.Bacc("TRN2", target_bir_lowering=False, num_devices=1)
    arrays, args = {}, []
    for name in INPUTS:
        a = np.ascontiguousarray(inputs[name])
        arrays[f"in_{name}"] = a
        args.append(nc.dram_tensor(f"in_{name}", a.shape, mybir.dt.from_np(a.dtype), kind="ExternalInput").ap())
    args.append(nc.dram_tensor("out", (N, D), F32, kind="ExternalOutput").ap())
    build(nc, *args)
    return run_bass_kernel_spmd(nc, [arrays], core_ids=[0]).results[0]["out"]
```
